# Optimizing a Trainium2 kernel written in Bass

```python
import numpy as np
import jax
import jax.numpy as jnp

def _softmax(x, axis=-1):
    return jax.nn.softmax(x, axis=axis)

def _gelu(x):
    return jax.nn.gelu(x, approximate=True)

def _silu(x):
    return jax.nn.silu(x)

def _sigmoid(x):
    return jax.nn.sigmoid(x)

def _layernorm(x, axis=-1, eps=1e-05):
    m = jnp.mean(x, axis=axis, keepdims=True)
    v = jnp.var(x, axis=axis, keepdims=True)
    return (x - m) / jnp.sqrt(v + eps)

def _scatter_add(tgt, idx, src, axis=0):
    return tgt.at[idx].add(src)

def _segment_sum(src, seg, n):
    return jax.ops.segment_sum(src, seg, n)
kernel_name = 'mk_adj_resnorm_d2_adj_r2_f54ab3'

def setup_inputs(seed: int=0):
    np.random.seed(seed)
    _w = jnp.asarray

    def _rec_inputs():
        import jax
        import jax.numpy as jnp
        _gk = jax.random.key(seed)
        x = 7.22e-05 + 1 * jax.random.normal(jax.random.fold_in(_gk, 1), (16, 512, 128), jnp.float32)
        _a = jax.random.bernoulli(jax.random.fold_in(_gk, 2), 0.03125, (512, 512))
        _a = jnp.logical_or(_a, jnp.swapaxes(_a, -1, -2))
        _a = jnp.logical_or(_a, jnp.eye(512, dtype=bool))
        _af = _a.astype(jnp.float32)
        _af = _af * jax.random.uniform(jax.random.fold_in(_gk, 3), (512, 512), jnp.float32, 0.05, 0.000976562)
        adj = _af
        return (x, adj)
    x, adj = _rec_inputs()

    def _L0_gnn_setup():
        import jax, jax.numpy as jnp
        import numpy as np
        N_STEPS = 8
        SPATIAL_SCALE = 1.0
        key = jax.random.key(seed)
        ks = jax.random.split(key, 6)
        B, N, D = (32, 512, 128)
        x = jax.random.normal(ks[0], (B, N, D), dtype=jnp.float32)
        adj_mx = jax.random.uniform(ks[1], (N, N), dtype=jnp.float32) / N
        alpha_train = jnp.ones((N,), dtype=jnp.float32)
        w = jnp.eye(D, dtype=jnp.float32) + 0.01 * jax.random.normal(ks[2], (D, D), dtype=jnp.float32)
        d = jax.random.uniform(ks[3], (D,), dtype=jnp.float32)
        fc_in_w = jax.random.normal(ks[4], (D, D), dtype=jnp.float32) * (1.0 / np.sqrt(D))
        fc_in_b = jnp.zeros((D,), dtype=jnp.float32)
        return {'x': x, 'adj_mx': adj_mx, 'alpha_train': alpha_train, 'w': w, 'd': d, 'fc_in_w': fc_in_w, 'fc_in_b': fc_in_b, 'vt': 0}
    _L0_gnn_all = _L0_gnn_setup()
    _L0_gnn_in = {k: v for k, v in _L0_gnn_all.items() if k in ('alpha_train', 'w', 'd', 'fc_in_w', 'fc_in_b')}
    del _L0_gnn_all

    def _L1_gnn_setup():
        import jax, jax.numpy as jnp
        import numpy as np
        BT, N, D, HEADS, E = (512, 64, 128, 4, 256)
        LRELU_SLOPE = 0.2
        EPS = 1e-08
        key = jax.random.key(seed)
        ks = jax.random.split(key, 8)
        d = D
        return {'H': jax.random.normal(ks[0], (BT, N, d), jnp.float32), 'W_lin': jax.random.normal(ks[1], (d, d), jnp.float32) / np.sqrt(d).astype(np.float32), 'W_val': jax.random.normal(ks[2], (d, d), jnp.float32) / np.sqrt(d).astype(np.float32), 'a': jax.random.normal(ks[3], (HEADS, d // HEADS), jnp.float32), 'W_out': jax.random.normal(ks[4], (d, d), jnp.float32) / np.sqrt(d).astype(np.float32), 'A0': jax.random.uniform(ks[5], (N, N), jnp.float32), 'src': jax.random.randint(ks[6], (E,), 0, N, jnp.int32), 'dst': jax.random.randint(ks[7], (E,), 0, N, jnp.int32)}
    _L1_gnn_all = _L1_gnn_setup()
    _L1_gnn_in = {k: v for k, v in _L1_gnn_all.items() if k in ('W_lin', 'W_val', 'a', 'W_out', 'src', 'dst')}
    del _L1_gnn_all
    return {'x': x, 'adj': adj, 'L0_gnn_alpha_train': _L0_gnn_in['alpha_train'], 'L0_gnn_w': _L0_gnn_in['w'], 'L0_gnn_d': _L0_gnn_in['d'], 'L0_gnn_fc_in_w': _L0_gnn_in['fc_in_w'], 'L0_gnn_fc_in_b': _L0_gnn_in['fc_in_b'], 'L1_gnn_W_lin': _L1_gnn_in['W_lin'], 'L1_gnn_W_val': _L1_gnn_in['W_val'], 'L1_gnn_a': _L1_gnn_in['a'], 'L1_gnn_W_out': _L1_gnn_in['W_out'], 'L1_gnn_src': _L1_gnn_in['src'], 'L1_gnn_dst': _L1_gnn_in['dst']}

def reference(x, adj, L0_gnn_alpha_train, L0_gnn_w, L0_gnn_d, L0_gnn_fc_in_w, L0_gnn_fc_in_b, L1_gnn_W_lin, L1_gnn_W_val, L1_gnn_a, L1_gnn_W_out, L1_gnn_src, L1_gnn_dst):
    import jax
    import jax.numpy as jnp

    def _L0_gnn_ref(x, adj_mx, alpha_train, w, d, fc_in_w, fc_in_b, vt):
        import jax, jax.numpy as jnp
        import numpy as np
        N_STEPS = 8
        SPATIAL_SCALE = 1.0
        x0 = jax.lax.stop_gradient(x)
        h = jnp.einsum('bnd,ed->bne', x, fc_in_w) + fc_in_b
        alph = jax.nn.sigmoid(alpha_train)[:, None]
        d_clamped = jnp.clip(d, 0.0, 1.0)
        w_eff = w * d_clamped @ w.T
        dt = jnp.float32(SPATIAL_SCALE / N_STEPS)

        def euler_step(h, _):
            ax = jnp.einsum('nm,bmd->bnd', adj_mx, h)
            f = alph * 0.5 * (ax - h) + h @ w_eff - h + x0
            return (h + dt * f, None)
        h, _ = jax.lax.scan(euler_step, h, None, length=N_STEPS)
        return h

    def _L1_gnn_ref(H, W_lin, W_val, a, W_out, A0, src, dst):
        import jax, jax.numpy as jnp
        import numpy as np
        BT, N, D, HEADS, E = (512, 64, 128, 4, 256)
        LRELU_SLOPE = 0.2
        EPS = 1e-08
        bt, n, d = H.shape
        h, dh = a.shape
        Xq = (H @ W_lin.T).reshape(bt, n, h, dh)
        Xv = (H @ W_val.T).reshape(bt, n, h, dh)
        Qs = Xq[:, src]
        Kt = Xq[:, dst]
        e = jnp.einsum('behd,hd->beh', jax.nn.leaky_relu(Qs + Kt, LRELU_SLOPE), a)
        e = e + jnp.log(A0[src, dst] + EPS)[None, :, None]
        e_t = e.transpose(1, 0, 2)
        m = jax.ops.segment_max(e_t, src, num_segments=n)
        ex = jnp.exp(e_t - m[src])
        denom = jax.ops.segment_sum(ex, src, num_segments=n)
        attn = ex / denom[src]
        Vt = Xv[:, dst].transpose(1, 0, 2, 3)
        Y = jax.ops.segment_sum(attn[..., None] * Vt, src, num_segments=n)
        Y = Y.transpose(1, 0, 2, 3).reshape(bt, n, d)
        return Y @ W_out.T
    x = _layernorm(x + _L0_gnn_ref(x, adj, L0_gnn_alpha_train, L0_gnn_w, L0_gnn_d, L0_gnn_fc_in_w, L0_gnn_fc_in_b, 0), axis=-1)
    x = _layernorm(x + _L1_gnn_ref(x, L1_gnn_W_lin, L1_gnn_W_val, L1_gnn_a, L1_gnn_W_out, adj, L1_gnn_src, L1_gnn_dst), axis=-1)
    return x

_drawn_inputs = setup_inputs


def setup_inputs(seed=0):
    import zlib

    import numpy as np

    out = dict(_drawn_inputs(seed))
    spreads = {'L0_gnn_alpha_train': (1.0, 0.2), 'L0_gnn_fc_in_b': (0.0, 0.1)}
    factors = {}
    for name, (base, spread) in spreads.items():
        noise = np.random.default_rng([zlib.crc32(name.encode()), seed]).standard_normal(out[name].shape)
        drawn = base * np.exp(spread * noise) if base else spread * noise
        out[name] = jnp.asarray(drawn.astype(out[name].dtype))
    for name, factor in factors.items():
        out[name] = (out[name] * factor).astype(out[name].dtype)
    return out
```

```python
from contextlib import ExitStack
from math import comb

import concourse.bass as bass
from concourse import mybir

F32 = mybir.dt.float32
F32R = mybir.dt.float32r
I32 = mybir.dt.int32
U32 = mybir.dt.uint32
ALU = mybir.AluOpType
ACT = mybir.ActivationFunctionType

P = 128
STEPS = 8
DT = 1.0 / STEPS
LN_EPS = 1e-5
LOG_EPS = 1e-8
LRELU = 0.2
LOWEST = -3.0e38
BABY = 3


def graph_kernel(nc, x, adj, alpha, w, d, fc_w, fc_b, W_lin, W_val, a, W_out, src, dst, out):
    B, N, D = x.shape
    H, DH = a.shape
    E = src.shape[0]
    NT = N // P
    ET = E // P
    CB = 512 // D
    CHUNKS = B // CB
    W = CB * D
    BH = CB * H
    K = STEPS + 1
    assert D == P and H * DH == D and N == 512 and W == 512 and 2 * E == 512 and K == BABY * BABY
    S_JOB, OUT_JOB, LEFT_JOBS = 3 * CB, 3 * CB + NT, 3 * CB + 2 * NT
    PAIRS = NT // 2
    R_JOBS = CB * PAIRS
    SM = 9

    x_v = x.rearrange("(c b) (t p) d -> c t p b d", b=CB, p=P)
    out_v = out.rearrange("(c b) (t p) d -> c t p b d", b=CB, p=P)
    adj_v = adj.rearrange("(t p) m -> t p m", p=P)

    ctx = ExitStack()
    with ctx:
        def sb(name, shape, dt=F32):
            return ctx.enter_context(nc.sbuf_tensor(name, shape, dt))

        def sem(name):
            return ctx.enter_context(nc.semaphore(name))

        p1h, p1l = sb("p1h", [P, NT, N], F32R), sb("p1l", [P, NT, N], F32R)
        p2h, p2l = sb("p2h", [P, NT, N], F32R), sb("p2l", [P, NT, N], F32R)
        p3h, p3l = sb("p3h", [P, NT, N], F32R), sb("p3l", [P, NT, N], F32R)
        xraw = sb("xraw", [P, NT, W])
        xh, xl = sb("xh", [P, 2, NT, D], F32R), sb("xl", [P, 2, NT, D], F32R)
        kth, ktl = sb("kth", [P, 2, BABY, N], F32R), sb("ktl", [P, 2, BABY, N], F32R)
        y0, y1 = sb("y0", [P, NT, W]), sb("y1", [P, NT, W])
        y2h, y2l = sb("y2h", [P, NT, W], F32R), sb("y2l", [P, NT, W], F32R)
        sh, sl = sb("sh", [P, NT, W], F32R), sb("sl", [P, NT, W], F32R)
        x1 = sb("x1", [P, NT, W])
        rh, rl = sb("rh", [P, BABY, BABY * D], F32R), sb("rl", [P, BABY, BABY * D], F32R)
        bias = sb("bias", [P, NT, D])
        pick = sb("pick", [P, NT, 2 * E], F32R)
        onesrc = sb("onesrc", [P, ET, N], F32R)
        gh, gl = sb("gh", [P, 2, 2 * E], F32R), sb("gl", [P, 2, 2 * E], F32R)
        tv = sb("tv", [P, 2 * W * 2])
        avh, avl = sb("avh", [P, CB, E], F32R), sb("avl", [P, CB, E], F32R)
        wh, wl = sb("wh", [P, 3, D], F32R), sb("wl", [P, 3, D], F32R)
        apad = sb("apad", [P, CB * BH])
        headrow = sb("headrow", [BH, CB, D])
        logrow = sb("logrow", [BH, E])
        seg = sb("seg", [BH, E + 1])
        same = sb("same", [BH, E])
        sme, smf, smg = sb("sme", [BH, E]), sb("smf", [BH, E]), sb("smg", [BH, E])
        ident = sb("ident", [P, P])
        st = sb("st", [P, 2, CB, 6])
        both, apart = sb("both", [P, 2, CB, 2]), sb("apart", [P, 2, CB])
        mean = sb("mean", [P, 2, NT, CB])
        ve = sb("ve", [P, 2, NT, CB])
        rstd = sb("rstd", [P, 2, NT, CB])
        nhalf = sb("nhalf", [P, CB])
        small = sb("small", [P, 96])

        tt = tv[:, 0:CB * E].rearrange("p (b e) -> p b e", b=CB)
        vv = tv[:, CB * E:2 * CB * E].rearrange("p (b e) -> p b e", b=CB)
        r2 = tv[:, 0:NT * W].rearrange("p (t w) -> p t w", t=NT)
        uh, ul = gh, gl
        x1h, x1l = sh, sl

        pn = x1
        pnh, pnl = y2h, y2l
        y0f = y0[:, :, :].rearrange("p t w -> p (t w)")
        y1f = y1[:, :, :].rearrange("p t w -> p (t w)")
        qp = y0f[:, 0:K * D].rearrange("p (i e) -> p i e", i=K)
        rf = y1f[:, 0:K * D].rearrange("p (j i e) -> p j i e", j=BABY, i=BABY)
        wt = y1f[:, K * D:K * D + D]
        wtd = y1f[:, K * D + D:K * D + 2 * D]
        nat = y0f[:, K * D:K * D + 5 * D].rearrange("p (i e) -> p i e", i=5)
        edge_ops = tv
        iota_row = edge_ops[:, 0:N]
        rows_i = edge_ops[:, N:N + 2 * E].bitcast(I32)
        perm = edge_ops[:, N:N + ET * E].rearrange("p (t r) -> p t r", t=ET)
        rows_f = edge_ops[:, 2 * N:2 * N + 2 * E]
        rep = edge_ops[:, 3 * N:3 * N + 2 * ET * P].rearrange("p (s t q) -> p s t q", s=2, t=ET)
        alpha_c, exp_c, half_c, diag_c = (small[:, 4 * i:4 * i + 4] for i in range(4))
        d_c, b_c, a_c = small[:, 16:17], small[:, 17:18], small[:, 18:19]
        iota_c = small[:, 20:24]
        cols_i = small[:, 24:28].bitcast(I32)
        cols_f = small[:, 28:32]
        key_c = small[:, 32:34]
        rank_c = small[:, 34:36]
        sorted_c = small[:, 36:40].rearrange("p (t s) -> p t s", t=ET)
        idx_f = small[:, 40:42]
        idx_u = small[:, 42:44].bitcast(U32)
        a_edge = small[:, 44:46]
        log_c = small[:, 46:48]
        c_t = small[:, 48:48 + K]
        log_rep = small[:, 60:92].rearrange("p (t q) -> p t q", t=ET)
        ones = sb("ones", [P, P])
        uc = sb("uc", [P, NT, K])
        us_h, us_l = sb("us_h", [P, 4, NT, 4], F32R), sb("us_l", [P, 4, NT, 4], F32R)
        uct = sb("uct", [K, P])
        ucr = y1f[0:K, 11 * D:11 * D + NT * P].rearrange("p (t q) -> p t q", t=NT)

        left = [ctx.enter_context(nc.psum_tensor(f"left{i}", [P, 512], F32)) for i in range(2)]
        yps = ctx.enter_context(nc.psum_tensor("yps", [P, 4, 512], F32))
        att = [ctx.enter_context(nc.psum_tensor(f"att{i}", [P, 512], F32)) for i in range(2)]

        adj_loaded, alpha_loaded, gnn_loaded = sem("adj_loaded"), sem("alpha_loaded"), sem("gnn_loaded")
        att_loaded, edges_loaded = sem("att_loaded"), sem("edges_loaded")
        consts = sem("consts")
        const_step = sem("const_step")
        dve_step = sem("dve_step")
        exp_alpha = sem("exp_alpha")
        keys_ranked = sem("keys_ranked")
        rows_sorted, cols_sorted = sem("rows_sorted"), sem("cols_sorted")
        cols_copied, idx_ready, adj_picked, logs = sem("cols_copied"), sem("idx_ready"), sem("adj_picked"), sem("logs")
        log_rep_ready, log_row_ready = sem("log_rep_ready"), sem("log_row_ready")
        w_turned, w_hi, w_lo, wt_ready = sem("w_turned"), sem("w_hi"), sem("w_lo"), sem("wt_ready")
        q_product, q_copied = sem("q_product"), sem("q_copied")
        m_ready, r_done, r_hi, r_lo = sem("m_ready"), sem("r_done"), sem("r_hi"), sem("r_lo")
        pn_ready, pn_hi, pn_lo = sem("pn_ready"), sem("pn_hi"), sem("pn_lo")
        pow_ready, pow_hi, pow_lo = sem("pow_ready"), sem("pow_hi"), sem("pow_lo")
        u_ready, u_split = sem("u_ready"), sem("u_split")
        c_ready, c_copied = sem("c_ready"), sem("c_copied")
        turned_uc, uc_rows, bias_ready, bias_copied = sem("turned_uc"), sem("uc_rows"), sem("bias_ready"), sem("bias_copied")
        onehots = sem("onehots")
        x_loaded = sem("x_loaded")
        x_free = sem("x_free")
        x_hi, x_lo = sem("x_hi"), sem("x_lo")
        left_ready, left_free = sem("left_ready"), sem("left_free")
        left_hi = sem("left_hi")
        y_ready, y_copied, y_free = sem("y_ready"), sem("y_copied"), sem("y_free")
        s_hi, s_lo = sem("s_hi"), sem("s_lo")
        ln_stats = [sem("ln1_stats"), sem("ln2_stats")]
        ln_halves = [sem("ln1_halves"), sem("ln2_halves")]
        ln_mean = [sem("ln1_mean"), sem("ln2_mean")]
        ln_var = [sem("ln1_var"), sem("ln2_var")]
        ln_rstd = [sem("ln1_rstd"), sem("ln2_rstd")]
        ln_done = [sem("ln1_done"), sem("ln2_done")]
        x1_hi, x1_lo = sem("x1_hi"), sem("x1_lo")
        g_ready, g_hi, g_lo = sem("g_ready"), sem("g_hi"), sem("g_lo")
        lin_ready = sem("lin_ready")
        q_scaled, q_leaky, v_copied = sem("q_scaled"), sem("q_leaky"), sem("v_copied")
        score_ready, sm_step, sm_exp = sem("score_ready"), sem("sm_step"), sem("sm_exp")
        head_ready, av_ready, av_hi, av_lo = sem("head_ready"), sem("av_ready"), sem("av_hi"), sem("av_lo")
        u2_ready, u2_hi, u2_lo = sem("u2_ready"), sem("u2_hi"), sem("u2_lo")
        z_ready, z_sum = sem("z_ready"), sem("z_sum")
        stored = sem("stored")
        tv_free = sem("tv_free")

        def need(eng, s, value):
            if not isinstance(value, int) or value > 0:
                eng.wait_ge(s, value)

        def passes(h1, l1, h2, l2):
            return ((h1, h2), (h1, l2), (l1, h2))

        def chunks(eng, body):
            body(0, True, False)
            with eng.Fori(1, CHUNKS) as c:
                body(c, True, True)
            body(CHUNKS, False, True)

        block = ctx.enter_context(nc.Block())

        @block.sync
        def _(sp):
            for t in range(NT):
                sp.dma_start(pn[:, t, :], adj_v[t]).then_inc(adj_loaded, 16)

            def load_x(c):
                need(sp, left_ready, LEFT_JOBS * (c - 1) + 3 * (CB - 1) + 1 if not isinstance(c, int) or c else 0)
                sp.sem_inc(x_free, 1)
                need(sp, x_lo, CB * c)
                sp.sem_inc(x_free, 1)
                for t in range(NT):
                    sp.dma_start(xraw[:, t, :].rearrange("p (b d) -> p b d", b=CB), x_v[c, t]).then_inc(x_loaded, 16)

            def body(c, diffuse, attend):
                if diffuse:
                    load_x(c)
                if attend:
                    for t in range(NT):
                        sp.wait_ge(ln_done[1], NT * (c - 1) + t + 1)
                        sp.dma_start(out_v[c - 1, t], r2[:, t, :].rearrange("p (b d) -> p b d", b=CB)).then_inc(stored, 16)
                    sp.wait_ge(stored, 16 * NT * c)
                    sp.sem_inc(tv_free, 1)

            chunks(sp, body)

        @block.gpsimd
        def _(pool):
            pool.memset(ident[:, :], 0.0).then_inc(const_step, 1)
            pool.memset(headrow[:, :, :], 1.0).then_inc(const_step, 1)
            pool.iota(iota_row, pattern=[[1, N]], base=0, channel_multiplier=0,
                      allow_small_or_imprecise_dtypes=True).then_inc(consts, 1)
            pool.iota(iota_c, pattern=[[P, NT]], base=0, channel_multiplier=1,
                      allow_small_or_imprecise_dtypes=True).then_inc(consts, 1)
            pool.wait_ge(const_step, 2)
            pool.affine_select(out=ident[:, :], in_=ident[:, :], compare_op=ALU.not_equal, fill=1.0,
                               base=0, pattern=[[-1, P]], channel_multiplier=1).then_inc(consts, 1)
            pool.affine_select(out=headrow[:, :, :].rearrange("q b (h e) -> q b h e", h=H),
                               in_=headrow[:, :, :].rearrange("q b (h e) -> q b h e", h=H),
                               compare_op=ALU.is_equal, fill=0.0,
                               base=0, pattern=[[-H, CB], [-1, H], [0, DH]], channel_multiplier=1).then_inc(consts, 1)
            pool.memset(nhalf[:, :], -0.5).then_inc(consts, 1)
            for t in range(NT):
                pool.wait_ge(pn_hi, t + 1)
                pool.tensor_tensor(pnl[:, t, :], pn[:, t, :], pnh[:, t, :].bitcast(F32), ALU.subtract).then_inc(pn_lo, 1)
            pool.wait_ge(idx_ready, 1)
            adj_flat = adj.rearrange("n (m o) -> (n m) o", o=1)
            for t in range(ET):
                pool.indirect_dma_start(a_edge[:, t:t + 1], None, adj_flat,
                                        bass.IndirectOffsetOnAxis(ap=idx_u[:, t:t + 1], axis=0)).then_inc(adj_picked, 16)

            def split_x(c, b):
                pool.wait_ge(x_hi, CB * c + b + 1)
                pool.tensor_tensor(xl[:, b % 2, :, :], xraw[:, :, b * D:(b + 1) * D],
                                   xh[:, b % 2, :, :].bitcast(F32), ALU.subtract).then_inc(x_lo, 1)

            def rsqrt(k, cc, t):
                pool.wait_ge(ln_var[k], NT * cc + t + 1)
                pool.tensor_tensor(rstd[:, k, t, :], ve[:, k, t, :], nhalf[:, :], ALU.pow).then_inc(ln_rstd[k], 1)

            def body(c, diffuse, attend):
                if diffuse:
                    split_x(c, 0)
                    split_x(c, 1)
                if attend:
                    for t in range(NT):
                        rsqrt(0, c - 1, t)
                if diffuse:
                    split_x(c, 2)
                if attend:
                    for t in range(NT):
                        pool.wait_ge(x1_hi, NT * (c - 1) + t + 1)
                        pool.tensor_tensor(x1l[:, t, :], x1[:, t, :], x1h[:, t, :].bitcast(F32), ALU.subtract).then_inc(x1_lo, 1)
                if diffuse:
                    split_x(c, 3)
                if attend:
                    for p in range(2):
                        pool.wait_ge(av_hi, 2 * (c - 1) + p + 1)
                        pool.tensor_tensor(avl[:, 2 * p:2 * p + 2, :], vv[:, 2 * p:2 * p + 2, :],
                                           avh[:, 2 * p:2 * p + 2, :].bitcast(F32), ALU.subtract).then_inc(av_lo, 1)
                if diffuse:
                    for t in range(NT):
                        pool.wait_ge(s_hi, NT * c + t + 1)
                        pool.tensor_tensor(sl[:, t, :], y1[:, t, :], sh[:, t, :].bitcast(F32), ALU.subtract).then_inc(s_lo, 1)
                if attend:
                    for t in range(NT):
                        rsqrt(1, c - 1, t)

            chunks(pool, body)

        @block.scalar
        def _(act):
            col = "(p o) -> p o"
            act.dma_start(alpha_c, alpha.rearrange("(t p) -> p t", p=P), allow_slow_non_contiguous=True).then_inc(alpha_loaded, 16)
            for s, e in enumerate((src, dst)):
                act.dma_start(rows_i[:, s * E:(s + 1) * E], e.rearrange("(o e) -> o e", o=1).broadcast_to([P, E])).then_inc(edges_loaded, 16)
                act.dma_start(cols_i[:, 2 * s:2 * s + 2], e.rearrange("(t p) -> p t", p=P), allow_slow_non_contiguous=True).then_inc(edges_loaded, 16)
            act.dma_start(nat[:, 0, :], w).then_inc(gnn_loaded, 16)
            act.dma_start(d_c, d.rearrange(col, o=1)).then_inc(gnn_loaded, 16)
            act.dma_start(nat[:, 1, :], fc_w).then_inc(gnn_loaded, 16)
            act.dma_start(b_c, fc_b.rearrange(col, o=1)).then_inc(gnn_loaded, 16)
            for i, m in enumerate((W_lin, W_val, W_out)):
                act.dma_start(nat[:, 2 + i, :], m).then_inc(att_loaded, 16)
            act.dma_start(a_c, a.rearrange("h (e o) -> (h e) o", o=1)).then_inc(att_loaded, 16)
            act.wait_ge(alpha_loaded, 16)
            act.activation(exp_c, alpha_c, ACT.Exp, scale=-1.0).then_inc(exp_alpha, 1)
            act.wait_ge(w_turned, 1)
            act.activation(wh[:, :, :].rearrange("p i e -> p (i e)"), att[0][:, D:4 * D], ACT.Copy).then_inc(w_hi, 1)
            act.wait_ge(q_product, 1)
            act.activation(qp[:, 1, :], left[0][:, 0:D], ACT.Copy, scale=DT).then_inc(q_copied, 1)
            for t in range(NT):
                act.wait_ge(pn_ready, t + 1)
                act.activation(pnh[:, t, :], pn[:, t, :], ACT.Copy).then_inc(pn_hi, 1)
            for i, m in enumerate((2, 3)):
                act.wait_ge(q_product, i + 2)
                act.activation(qp[:, m:2 * m - 1 if m == 3 else 3, :].rearrange("p i e -> p (i e)"),
                               left[0][:, D:2 * D] if m == 2 else left[0][:, 2 * D:4 * D], ACT.Copy).then_inc(q_copied, 1)
            for n, ph in enumerate((p1h, p2h, p3h)):
                for t in range(NT):
                    act.wait_ge(pow_ready, NT * n + t + 1)
                    act.activation(ph[:, t, :], yps[:, t, :], ACT.Copy).then_inc(pow_hi, 1)
                if n == 0:
                    act.wait_ge(q_product, 4)
                    act.activation(qp[:, 5:9, :].rearrange("p i e -> p (i e)"), left[1][:, :], ACT.Copy).then_inc(q_copied, 1)
            act.wait_ge(r_done, 1)
            act.activation(rh[:, :, :], rf[:, :, :, :].rearrange("p j i e -> p j (i e)"), ACT.Copy).then_inc(r_hi, 1)
            act.wait_ge(adj_picked, 16 * ET)
            act.wait_ge(consts, 6)
            act.activation(log_c, a_edge, ACT.Ln, bias=small[:, 92:93]).then_inc(logs, 1)

            def split_x(c, b):
                need(act, left_ready, (LEFT_JOBS * c + 3 * (b - 2) + 3) if b >= 2 else 0)
                act.activation(xh[:, b % 2, :, :], xraw[:, :, b * D:(b + 1) * D], ACT.Copy).then_inc(x_hi, 1)

            def baby_hi(c, b):
                need(act, y_ready, R_JOBS * c + PAIRS * (b - 1))
                for j in range(BABY):
                    act.wait_ge(left_ready, LEFT_JOBS * c + 3 * b + j + 1)
                    act.activation(kth[:, b % 2, j, :], left[(3 * b + j) % 2][:, :], ACT.Copy).then_inc(left_hi, 1)

            def y_copy(c, b):
                for p in range(PAIRS):
                    act.wait_ge(y_ready, R_JOBS * c + PAIRS * b + p + 1)
                    ps = yps[:, 2 * p:2 * p + 2, :]
                    act.activation(y2h[:, 2 * p:2 * p + 2, b * D:(b + 1) * D], ps[:, :, 2 * D:3 * D], ACT.Copy)
                    act.activation(y1[:, 2 * p:2 * p + 2, b * D:(b + 1) * D], ps[:, :, D:2 * D], ACT.Copy).then_inc(y_copied, 1)

            def gather_hi(cc, p):
                if p:
                    act.wait_ge(lin_ready, 4 * cc + 2)
                for b in (2 * p, 2 * p + 1):
                    act.wait_ge(g_ready, CB * cc + b + 1)
                    act.activation(gh[:, b % 2, :], att[b % 2][:, :], ACT.Copy).then_inc(g_hi, 1)

            def lin(cc, p):
                if p == 0:
                    act.wait_ge(tv_free, cc + 1)
                act.wait_ge(lin_ready, 4 * cc + 2 * p + 1)
                act.activation(tt[:, 2 * p:2 * p + 2, :], att[0][:, :].rearrange("p (b e) -> p b e", b=2),
                               ACT.Copy, scale=LRELU).then_inc(q_scaled, 1)
                act.wait_ge(lin_ready, 4 * cc + 2 * p + 2)
                act.activation(vv[:, 2 * p:2 * p + 2, :], att[1][:, :].rearrange("p (b e) -> p b e", b=2),
                               ACT.Copy).then_inc(v_copied, 1)

            def s_split(c, t):
                act.wait_ge(left_free, LEFT_JOBS * c + S_JOB + t + 1)
                act.activation(sh[:, t, :], y1[:, t, :], ACT.Copy).then_inc(s_hi, 1)

            def body(c, diffuse, attend):
                if diffuse:
                    act.wait_ge(x_loaded, 16 * NT * (c + 1))
                    need(act, left_ready, LEFT_JOBS * (c - 1) + S_JOB if not isinstance(c, int) or c else 0)
                    split_x(c, 0)
                    split_x(c, 1)
                    baby_hi(c, 0)
                    split_x(c, 2)
                if attend:
                    act.wait_ge(left_ready, LEFT_JOBS * c)
                    for t in range(NT):
                        act.wait_ge(ln_done[0], NT * (c - 1) + t + 1)
                        act.activation(x1h[:, t, :], x1[:, t, :], ACT.Copy).then_inc(x1_hi, 1)
                if diffuse:
                    baby_hi(c, 1)
                    split_x(c, 3)
                if attend:
                    gather_hi(c - 1, 0)
                if diffuse:
                    y_copy(c, 0)
                if attend:
                    lin(c - 1, 0)
                if diffuse:
                    baby_hi(c, 2)
                if attend:
                    gather_hi(c - 1, 1)
                if diffuse:
                    y_copy(c, 1)
                if attend:
                    lin(c - 1, 1)
                if diffuse:
                    baby_hi(c, 3)
                    y_copy(c, 2)
                if attend:
                    act.wait_ge(sm_step, SM * (c - 1) + 4)
                    act.activation(smf[:, :], smg[:, :], ACT.Exp).then_inc(sm_exp, 1)
                if diffuse:
                    y_copy(c, 3)
                if attend:
                    for p in range(2):
                        act.wait_ge(av_ready, 2 * (c - 1) + p + 1)
                        act.activation(avh[:, 2 * p:2 * p + 2, :], vv[:, 2 * p:2 * p + 2, :], ACT.Copy).then_inc(av_hi, 1)
                if diffuse:
                    s_split(c, 0)
                    s_split(c, 1)
                if attend:
                    for t in range(ET):
                        act.wait_ge(u2_ready, ET * (c - 1) + t + 1)
                        act.activation(uh[:, t, :], att[t][:, :], ACT.Copy).then_inc(u2_hi, 1)
                if diffuse:
                    s_split(c, 2)
                    s_split(c, 3)

            chunks(act, body)

        @block.tensor
        def _(pe):
            pe.wait_ge(consts, 6)
            pe.wait_ge(gnn_loaded, 64)
            pe.wait_ge(att_loaded, 64)
            for i, m in enumerate((0, 2, 3, 4)):
                mm = pe.transpose(att[0][:, i * D:(i + 1) * D], nat[:, m, :], ident[:, :])
            mm.then_inc(w_turned, 1)
            pe.wait_ge(keys_ranked, 1)
            for s in range(2):
                for t in range(ET):
                    mm = pe.matmul(att[1][:, s * E:(s + 1) * E], rep[:, s, t, :], perm[:, t, :],
                                   start=(t == 0), stop=(t == ET - 1))
            mm.then_inc(rows_sorted, 1)
            for r in range(ET):
                for t in range(ET):
                    mm = pe.matmul(left[1][:, 2 * r:2 * r + 2], perm[:, t, r * P:(r + 1) * P], cols_f[:, t::2],
                                   start=(t == 0), stop=(t == ET - 1))
            mm.then_inc(cols_sorted, 1)
            pe.wait_ge(wt_ready, 1)
            pe.matmul(left[0][:, 0:D], wtd, wt, start=True, stop=True).then_inc(q_product, 1)
            for t in range(NT):
                pe.wait_ge(pn_ready, NT)
                for n in range(NT):
                    mm = pe.transpose(yps[:, t, n * P:(n + 1) * P], pn[:, n, t * P:(t + 1) * P], ident[:, :])
                mm.then_inc(pow_ready, 1)
                if t == 0:
                    pe.wait_ge(q_copied, 1)
                    pe.matmul(left[0][:, D:2 * D], qp[:, 1, :], qp[:, 1, :], start=True, stop=True).then_inc(q_product, 1)
                if t == 3:
                    pe.wait_ge(q_copied, 2)
                    pe.matmul(left[0][:, 2 * D:4 * D], qp[:, 2, :], qp[:, 1:3, :].rearrange("p i e -> p (i e)"),
                              start=True, stop=True).then_inc(q_product, 1)
            pe.wait_ge(q_copied, 3)
            pe.wait_ge(cols_copied, 1)
            pe.matmul(left[1][:, :], qp[:, 4, :], qp[:, 1:5, :].rearrange("p i e -> p (i e)"),
                      start=True, stop=True).then_inc(q_product, 1)

            def power(n, ph, pl):
                pe.wait_ge(pow_lo, NT * (n - 1))
                for t in range(NT):
                    todo = [q for k in range(NT) for q in passes(pnh[:, k, t * P:(t + 1) * P], pnl[:, k, t * P:(t + 1) * P],
                                                                 ph[:, k, :], pl[:, k, :])]
                    for i, (l, r) in enumerate(todo):
                        mm = pe.matmul(yps[:, t, :], l, r, start=(i == 0), stop=(i == len(todo) - 1))
                    mm.then_inc(pow_ready, 1)

            def u_step(s, ph, pl):
                pe.wait_ge(u_split, s + 1)
                for n in range(NT):
                    todo = [q for m in range(NT) for q in passes(ph[:, m, n * P:(n + 1) * P], pl[:, m, n * P:(n + 1) * P],
                                                                 us_h[:, s, m, :], us_l[:, s, m, :])]
                    for i, (l, r) in enumerate(todo):
                        mm = pe.matmul(att[1][:, 4 * n:4 * n + 4], l, r, start=(i == 0), stop=(i == len(todo) - 1))
                mm.then_inc(u_ready, 1)

            pe.wait_ge(pn_lo, NT)
            power(2, p1h, p1l)
            pe.wait_ge(onehots, 1)
            u_step(0, p1h, p1l)
            pe.wait_ge(q_copied, 4)
            pe.wait_ge(w_lo, 1)
            for i, ps in enumerate((left[0], left[1], att[0])):
                mm = pe.matmul(ps[:, 0:BABY * D], nat[:, 1, :], qp[:, BABY * i:BABY * i + BABY, :].rearrange("p i e -> p (i e)"),
                               start=True, stop=True)
            mm.then_inc(m_ready, 1)
            power(3, p2h, p2l)
            pe.wait_ge(u_split, 2)
            for i in range(K):
                mm = pe.matmul(att[1][:, 32 + i:33 + i], qp[:, i, :], b_c, start=True, stop=True)
            mm.then_inc(c_ready, 1)
            u_step(1, p1h, p1l)
            pe.wait_ge(pow_lo, 3 * NT)
            u_step(2, p3h, p3l)
            pe.wait_ge(log_rep_ready, 1)
            for t in range(ET):
                mm = pe.matmul(left[1][0:BH, t * P:(t + 1) * P], log_rep[:, t, :], ident[:, :], start=True, stop=True)
            mm.then_inc(log_row_ready, 1)
            u_step(3, p3h, p3l)
            pe.wait_ge(u_split, 5)
            pe.wait_ge(c_copied, 1)
            for t in range(NT):
                pe.matmul(att[0][0:K, t * P:(t + 1) * P], uc[:, t, :], ident[:, :], start=True, stop=True)
            pe.matmul(left[0][0:K, 0:P], c_t, ident[:, :], start=True, stop=True).then_inc(turned_uc, 1)
            pe.wait_ge(uc_rows, 1)
            for t in range(NT):
                mm = pe.matmul(att[1][:, t * P:(t + 1) * P], ucr[:, t, :], uct[:, :], start=True, stop=True)
            mm.then_inc(bias_ready, 1)
            pe.wait_ge(r_lo, 1)
            pe.wait_ge(bias_copied, 1)

            def left_bank(c, job):
                need(pe, left_free, LEFT_JOBS * c + job - 1)
                return left[job % 2]

            def baby(c, b):
                pe.wait_ge(x_lo, CB * c + b + 1)
                ps = left_bank(c, 3 * b)
                for t in range(NT):
                    mm = pe.transpose(ps[:, t * P:(t + 1) * P], xraw[:, t, b * D:(b + 1) * D], ident[:, :])
                mm.then_inc(left_ready, 1)
                for j, (ph, pl) in enumerate(((p1h, p1l), (p2h, p2l)), 1):
                    ps = left_bank(c, 3 * b + j)
                    todo = [q for m in range(NT) for q in passes(xh[:, b % 2, m, :], xl[:, b % 2, m, :], ph[:, m, :], pl[:, m, :])]
                    for i, (l, r) in enumerate(todo):
                        mm = pe.matmul(ps[:, :], l, r, start=(i == 0), stop=(i == len(todo) - 1))
                    mm.then_inc(left_ready, 1)

            def rights(c, b):
                pe.wait_ge(left_free, LEFT_JOBS * c + 3 * b + 3)
                for p in range(PAIRS):
                    need(pe, y_free, R_JOBS * c + PAIRS * b + p - 1)
                    for n in (2 * p, 2 * p + 1):
                        todo = [q for j in range(BABY) for q in passes(kth[:, b % 2, j, n * P:(n + 1) * P],
                                                                       ktl[:, b % 2, j, n * P:(n + 1) * P], rh[:, j, :], rl[:, j, :])]
                        for i, (l, r) in enumerate(todo):
                            mm = pe.matmul(yps[:, n, 0:BABY * D], l, r, start=(i == 0), stop=(i == len(todo) - 1))
                    mm.then_inc(y_ready, 1)

            def giant(c, job, n, zh, zl):
                ps = left_bank(c, job)
                todo = [q for m in range(NT) for q in passes(p3h[:, m, n * P:(n + 1) * P], p3l[:, m, n * P:(n + 1) * P],
                                                             zh[:, m, :], zl[:, m, :])]
                for i, (l, r) in enumerate(todo):
                    mm = pe.matmul(ps[:, :], l, r, start=(i == 0), stop=(i == len(todo) - 1))
                mm.then_inc(left_ready, 1)

            def gather(cc, p):
                for b in (2 * p, 2 * p + 1):
                    if p:
                        pe.wait_ge((q_leaky, v_copied)[b % 2], 2 * cc + 1)
                    for t in range(NT):
                        pe.matmul(att[b % 2][:, :], x1h[:, t, b * D:(b + 1) * D], pick[:, t, :], start=(t == 0), stop=False)
                        mm = pe.matmul(att[b % 2][:, :], x1l[:, t, b * D:(b + 1) * D], pick[:, t, :], start=False, stop=(t == NT - 1))
                    mm.then_inc(g_ready, 1)

            def lin(cc, p):
                pe.wait_ge(g_lo, CB * cc + 2 * p + 2)
                for i in range(2):
                    cols = slice(i * E, (i + 1) * E)
                    todo = passes(wh[:, i, :], wl[:, i, :], gh[:, :, cols], gl[:, :, cols])
                    for n, (l, r) in enumerate(todo):
                        mm = pe.matmul(att[i][:, :].rearrange("p (b e) -> p b e", b=2), l, r, start=(n == 0), stop=(n == 2))
                    mm.then_inc(lin_ready, 1)

            def body(c, diffuse, attend):
                if attend:
                    for t in range(NT):
                        if t == 0:
                            pe.wait_ge(s_lo, NT * c)
                        giant(c - 1, OUT_JOB + t, t, sh, sl)
                if diffuse:
                    baby(c, 0)
                    baby(c, 1)
                if attend:
                    pe.wait_ge(x1_lo, NT * c)
                    gather(c - 1, 0)
                if diffuse:
                    rights(c, 0)
                if attend:
                    lin(c - 1, 0)
                if diffuse:
                    baby(c, 2)
                if attend:
                    gather(c - 1, 1)
                if diffuse:
                    rights(c, 1)
                if attend:
                    lin(c - 1, 1)
                if diffuse:
                    baby(c, 3)
                if attend:
                    pe.wait_ge(q_leaky, 2 * c)
                    for b in range(CB):
                        mm = pe.matmul(att[0][0:BH, 0:E], apad[:, b * BH:(b + 1) * BH], tt[:, b, :], start=(b == 0), stop=(b == CB - 1))
                    mm.then_inc(score_ready, 1)
                if diffuse:
                    rights(c, 2)
                    rights(c, 3)
                if attend:
                    pe.wait_ge(sm_step, SM * c)
                    pe.wait_ge(v_copied, 2 * c)
                    for p in range(2):
                        for b in (2 * p, 2 * p + 1):
                            mm = pe.matmul(att[p][:, (b % 2) * E:(b % 2 + 1) * E], headrow[:, b, :], sme[:, :], start=True, stop=True)
                        mm.then_inc(head_ready, 1)
                if diffuse:
                    pe.wait_ge(y_free, R_JOBS * (c + 1))
                    giant(c, S_JOB, 0, y2h, y2l)
                    giant(c, S_JOB + 1, 1, y2h, y2l)
                if attend:
                    pe.wait_ge(av_lo, 2 * c)
                    for t in range(ET):
                        for b in range(CB):
                            es = slice(t * P, (t + 1) * P)
                            for n, (l, r) in enumerate(passes(avh[:, b, es], avl[:, b, es], wh[:, 2, :], wl[:, 2, :])):
                                mm = pe.matmul(att[t][:, b * D:(b + 1) * D], l, r, start=(n == 0), stop=(n == 2))
                        mm.then_inc(u2_ready, 1)
                if diffuse:
                    giant(c, S_JOB + 2, 2, y2h, y2l)
                    giant(c, S_JOB + 3, 3, y2h, y2l)
                if attend:
                    pe.wait_ge(u2_lo, ET * c)
                    for n in range(NT):
                        if n >= 2:
                            pe.wait_ge(z_sum, NT * (c - 1) + n - 1)
                        for t in range(ET):
                            pe.matmul(att[n % 2][:, :], onesrc[:, t, n * P:(n + 1) * P], uh[:, t, :], start=(t == 0), stop=False)
                            mm = pe.matmul(att[n % 2][:, :], onesrc[:, t, n * P:(n + 1) * P], ul[:, t, :], start=False, stop=(t == ET - 1))
                        mm.then_inc(z_ready, 1)

            chunks(pe, body)

        @block.vector
        def _(dve):
            done = [0]

            def link(ins):
                done[0] += 1
                ins.then_inc(dve_step, 1)
                dve.wait_ge(dve_step, done[0])

            dve.memset(ones[:, :], 1.0)
            dve.memset(us_h[:, :, :, :].rearrange("p s t c -> p (s t c)").bitcast(F32), 0.0)
            dve.memset(us_l[:, :, :, :].rearrange("p s t c -> p (s t c)").bitcast(F32), 0.0)
            dve.memset(apad[:, :], 0.0)
            dve.memset(seg[:, :], LOWEST)
            dve.memset(same[:, :], 0.0)
            dve.memset(small[:, 92:93], LOG_EPS).then_inc(consts, 1)
            link(dve.memset(uc[:, :, K - 1:K], 1.0))
            link(dve.tensor_copy(us_h[:, 0, :, 0:1], uc[:, :, K - 1:K]))
            dve.wait_ge(edges_loaded, 64)
            dve.wait_ge(consts, 6)
            dve.tensor_copy(rows_f, rows_i)
            link(dve.tensor_copy(cols_f, cols_i))
            dve.scalar_tensor_tensor(out=rows_f[:, 0:E], in0=rows_f[:, 0:E], scalar=float(E), in1=iota_row[:, 0:E], op0=ALU.mult, op1=ALU.add)
            dve.scalar_tensor_tensor(out=key_c, in0=cols_f[:, 0:2], scalar=float(E), in1=iota_c[:, 0:2], op0=ALU.mult, op1=ALU.add)
            for s in range(2):
                for t in range(ET):
                    ins = dve.tensor_scalar(rep[:, s, t, :], ones[:, :], cols_f[:, 2 * s + t:2 * s + t + 1], None, ALU.mult)
            link(ins)
            for t in range(ET):
                ins = dve.tensor_scalar(rows_f[:, E:2 * E], rows_f[:, 0:E], key_c[:, t:t + 1], 0.0, ALU.is_lt, ALU.add,
                                        accum_out=rank_c[:, t:t + 1])
                link(ins)
            for t in range(ET):
                ins = dve.tensor_scalar(perm[:, t, :], iota_row[:, 0:E], rank_c[:, t:t + 1], None, ALU.is_equal)
            ins.then_inc(keys_ranked, 1)
            dve.wait_ge(exp_alpha, 1)
            link(dve.tensor_scalar(exp_c, exp_c, 1.0, None, ALU.add))
            link(dve.reciprocal(half_c, exp_c))
            link(dve.tensor_scalar(half_c, half_c, DT / 2, None, ALU.mult))
            link(dve.tensor_scalar(diag_c, half_c, -1.0, 1.0 - DT, ALU.mult, ALU.add))
            dve.wait_ge(w_hi, 1)
            dve.tensor_scalar(d_c, d_c, 0.0, 1.0, ALU.max, ALU.min)
            link(dve.tensor_copy(wt, att[0][:, 0:D]))
            dve.tensor_scalar(wtd, wt, d_c, None, ALU.mult).then_inc(wt_ready, 1)
            dve.wait_ge(adj_loaded, 16 * NT)
            for t in range(NT):
                ins = dve.tensor_scalar(pn[:, t, :], pn[:, t, :], half_c[:, t:t + 1], None, ALU.mult)
            link(ins)
            for t in range(NT):
                dg = pn[:, t, t * P:(t + 1) * P]
                dve.scalar_tensor_tensor(out=dg, in0=ident[:, :], scalar=diag_c[:, t:t + 1], in1=dg,
                                         op0=ALU.mult, op1=ALU.add).then_inc(pn_ready, 1)
            dve.wait_ge(cols_sorted, 1)
            link(dve.tensor_copy(sorted_c[:, :, :], left[1][:, 0:2 * ET].rearrange("p (t s) -> p t s", t=ET)))
            link(dve.scalar_tensor_tensor(out=idx_f, in0=sorted_c[:, :, 0], scalar=float(N), in1=sorted_c[:, :, 1],
                                          op0=ALU.mult, op1=ALU.add))
            dve.tensor_copy(idx_u, idx_f).then_inc(idx_ready, 1)
            dve.wait_ge(rows_sorted, 1)
            link(dve.tensor_copy(rows_f, att[1][:, :]))
            dve.sem_inc(cols_copied, 1)

            def power_lo(n, ph, pl):
                for t in range(NT):
                    dve.wait_ge(pow_hi, NT * n + t + 1)
                    dve.tensor_tensor(pl[:, t, :], yps[:, t, :], ph[:, t, :].bitcast(F32), ALU.subtract).then_inc(pow_lo, 1)

            power_lo(0, p1h, p1l)
            dve.tensor_tensor(wl[:, :, :].rearrange("p i e -> p (i e)"), att[0][:, D:4 * D],
                              wh[:, :, :].rearrange("p i e -> p (i e)").bitcast(F32), ALU.subtract).then_inc(w_lo, 1)
            link(dve.tensor_tensor(same[:, 1:E], rows_f[0:BH, 1:E], rows_f[0:BH, 0:E - 1], ALU.is_equal))
            dve.tensor_scalar(seg[:, 1:E], same[:, 1:E], -1.0, -LOWEST, ALU.add, ALU.mult)
            for t in range(NT):
                ins = dve.tensor_scalar(pick[:, t, E:2 * E], rows_f[:, E:2 * E], iota_c[:, t:t + 1], None, ALU.is_equal)
            link(ins)
            for t in range(NT):
                dve.scalar_tensor_tensor(out=pick[:, t, 0:E], in0=rows_f[:, 0:E], scalar=iota_c[:, t:t + 1],
                                         in1=pick[:, t, E:2 * E].bitcast(F32), op0=ALU.is_equal, op1=ALU.add)
            for t in range(ET):
                dve.tensor_scalar(onesrc[:, t, :], iota_row, sorted_c[:, t, 0:1], None, ALU.is_equal)
            for h in range(H):
                rows = slice(h * DH, (h + 1) * DH)
                ins = dve.tensor_scalar(apad[rows, h::BH + H], ones[rows, 0:CB], a_c[rows, :], None, ALU.mult)
            link(dve.tensor_copy(qp[:, 0, :], ident[:, :]))
            dve.sem_inc(onehots, 1)
            dve.sem_inc(u_split, 1)
            power_lo(1, p2h, p2l)

            def u_copy(s, n_cols, col):
                dve.wait_ge(u_ready, s + 1)
                ps = att[1][:, 0:4 * NT].rearrange("p (t c) -> p t c", t=NT)[:, :, 0:n_cols]
                link(dve.tensor_copy(uc[:, :, col:col + n_cols], ps))
                if s == 0:
                    part = uc[:, :, K - 2:K - 1]
                else:
                    part = uc[:, :, K - 3 * s:K - 3 * s + 3]
                if s < 3:
                    n = part.shape[2]
                    link(dve.tensor_copy(us_h[:, s + 1, :, 0:n], part))
                    link(dve.tensor_tensor(us_l[:, s + 1, :, 0:n], part, us_h[:, s + 1, :, 0:n].bitcast(F32), ALU.subtract))
                dve.sem_inc(u_split, 1)

            u_copy(0, 1, K - 2)
            dve.wait_ge(m_ready, 1)
            dve.wait_ge(q_copied, 4)
            for k in range(K):
                i = STEPS - k
                ps = (left[0], left[1], att[0])[i // BABY][:, (i % BABY) * D:(i % BABY + 1) * D]
                ins = dve.tensor_scalar(rf[:, k % BABY, k // BABY, :], ps, float(comb(STEPS, k)), None, ALU.mult)
            link(ins)
            for i in range(STEPS):
                for k in range(STEPS - i):
                    r = rf[:, k % BABY, k // BABY, :]
                    coef = DT * comb(i + k, k) + (1.0 if i == 0 and k == 0 else 0.0)
                    ins = dve.scalar_tensor_tensor(out=r, in0=qp[:, i, :], scalar=coef, in1=r, op0=ALU.mult, op1=ALU.add)
                link(ins)
            dve.sem_inc(r_done, 1)
            power_lo(2, p3h, p3l)
            dve.wait_ge(c_ready, 1)
            dve.wait_ge(u_ready, 2)
            for i in range(K):
                ins = dve.tensor_scalar(c_t[:, i:i + 1], att[1][:, 32 + i:33 + i], float(comb(STEPS, i)), None, ALU.mult)
            link(ins)
            dve.sem_inc(c_copied, 1)
            u_copy(1, 1, K - 3)
            dve.wait_ge(r_hi, 1)
            dve.tensor_tensor(rl[:, :, :].rearrange("p j e -> p (j e)"), rf[:, :, :, :].rearrange("p j i e -> p (j i e)"),
                              rh[:, :, :].rearrange("p j e -> p (j e)").bitcast(F32), ALU.subtract).then_inc(r_lo, 1)
            u_copy(2, 3, K - 6)
            dve.wait_ge(logs, 1)
            for t in range(ET):
                ins = dve.tensor_scalar(log_rep[:, t, :], ones[:, 0:BH], log_c[:, t:t + 1], None, ALU.mult)
            ins.then_inc(log_rep_ready, 1)
            u_copy(3, 3, 0)
            dve.wait_ge(log_row_ready, 1)
            dve.tensor_copy(logrow[:, :], left[1][0:BH, 0:E])
            dve.wait_ge(turned_uc, 1)
            dve.tensor_copy(ucr[:, :, :].rearrange("p t q -> p (t q)"), att[0][0:K, :])
            dve.tensor_copy(uct[:, :], left[0][0:K, 0:P]).then_inc(uc_rows, 1)
            dve.wait_ge(bias_ready, 1)
            dve.tensor_copy(bias[:, :, :].rearrange("p t e -> p (t e)"), att[1][:, :]).then_inc(bias_copied, 1)

            def baby_lo(c, b, js=range(BABY)):
                for j in js:
                    dve.wait_ge(left_hi, 3 * CB * c + 3 * b + j + 1)
                    dve.tensor_tensor(ktl[:, b % 2, j, :], left[(3 * b + j) % 2][:, :], kth[:, b % 2, j, :].bitcast(F32),
                                      ALU.subtract).then_inc(left_free, 1)

            def y_split(c, b, p):
                dve.wait_ge(y_copied, R_JOBS * c + PAIRS * b + p + 1)
                ps = yps[:, 2 * p:2 * p + 2, :]
                rows, cols = slice(2 * p, 2 * p + 2), slice(b * D, (b + 1) * D)
                dve.tensor_tensor(y2l[:, rows, cols], ps[:, :, 2 * D:3 * D], y2h[:, rows, cols].bitcast(F32), ALU.subtract)
                dve.tensor_tensor(y0[:, rows, cols], ps[:, :, 0:D], bias[:, rows, :], ALU.add).then_inc(y_free, 1)

            def s_add(c, t):
                job = S_JOB + t
                dve.wait_ge(left_ready, LEFT_JOBS * c + job + 1)
                dve.tensor_tensor(y1[:, t, :], left[job % 2][:, :], y1[:, t, :], ALU.add).then_inc(left_free, 1)

            def gather_lo(cc, p):
                for b in (2 * p, 2 * p + 1):
                    dve.wait_ge(g_hi, CB * cc + b + 1)
                    dve.tensor_tensor(gl[:, b % 2, :], att[b % 2][:, :], gh[:, b % 2, :].bitcast(F32), ALU.subtract).then_inc(g_lo, 1)

            def leaky(cc, p):
                dve.wait_ge(q_scaled, 2 * cc + p + 1)
                dve.tensor_tensor(tt[:, 2 * p:2 * p + 2, :], att[0][:, :].rearrange("p (b e) -> p b e", b=2),
                                  tt[:, 2 * p:2 * p + 2, :], ALU.max).then_inc(q_leaky, 1)

            def moments(k, cc, t, rows):
                for b in range(CB):
                    ins = dve.bn_stats(st[:, k, b, :], rows[:, b * D:(b + 1) * D])
                ins.then_inc(ln_stats[k], 1)
                dve.wait_ge(ln_stats[k], NT * cc + t + 1)
                dve.tensor_tensor(both[:, k, :, :], st[:, k, :, 1:3], st[:, k, :, 4:6], ALU.add)
                dve.tensor_tensor(apart[:, k, :], st[:, k, :, 1], st[:, k, :, 4], ALU.subtract).then_inc(ln_halves[k], 1)
                dve.wait_ge(ln_halves[k], NT * cc + t + 1)
                dve.scalar_tensor_tensor(out=apart[:, k, :], in0=apart[:, k, :], scalar=0.25, in1=apart[:, k, :],
                                         op0=ALU.mult, op1=ALU.mult)
                dve.tensor_scalar(ve[:, k, t, :], both[:, k, :, 1], 1.0 / D, LN_EPS, ALU.mult, ALU.add)
                dve.tensor_scalar(mean[:, k, t, :], both[:, k, :, 0], 0.5, None, ALU.mult).then_inc(ln_mean[k], 1)
                dve.wait_ge(ln_mean[k], NT * cc + t + 1)
                dve.tensor_tensor(ve[:, k, t, :], ve[:, k, t, :], apart[:, k, :], ALU.add).then_inc(ln_var[k], 1)

            def normalise(k, cc, t, rows):
                dve.wait_ge(ln_rstd[k], NT * cc + t + 1)
                for b in range(CB):
                    r = rows[:, b * D:(b + 1) * D]
                    ins = dve.tensor_scalar(r, r, mean[:, k, t, b:b + 1], rstd[:, k, t, b:b + 1], ALU.subtract, ALU.mult)
                ins.then_inc(ln_done[k], 1)

            def sm(cc, n, ins):
                ins.then_inc(sm_step, 1)
                dve.wait_ge(sm_step, SM * cc + n)

            def softmax_max(cc):
                dve.wait_ge(score_ready, cc + 1)
                sm(cc, 1, dve.tensor_tensor(sme[:, :], att[0][0:BH, 0:E], logrow[:, :], ALU.add))
                sm(cc, 2, dve.tensor_tensor_scan(smf[:, :], seg[:, 0:E], sme[:, :], LOWEST, ALU.add, ALU.max))
                sm(cc, 3, dve.tensor_tensor_scan(smg[:, ::-1], seg[:, E:0:-1], smf[:, ::-1], LOWEST, ALU.add, ALU.max))
                dve.tensor_tensor(smg[:, :], sme[:, :], smg[:, :], ALU.subtract).then_inc(sm_step, 1)

            def softmax_sum(cc):
                dve.wait_ge(sm_exp, cc + 1)
                sm(cc, 5, dve.tensor_tensor_scan(smg[:, :], same[:, :], smf[:, :], 0.0, ALU.mult, ALU.add))
                sm(cc, 6, dve.tensor_tensor_scan(sme[:, ::-1], seg[:, E:0:-1], smg[:, ::-1], LOWEST, ALU.add, ALU.max))
                sm(cc, 7, dve.reciprocal(smg[:, :], sme[:, :]))
                sm(cc, 8, dve.tensor_tensor(sme[:, :], smf[:, :], smg[:, :], ALU.mult))
                dve.sem_inc(sm_step, 1)

            def body(c, diffuse, attend):
                if attend:
                    for t in range(NT):
                        job = OUT_JOB + t
                        dve.wait_ge(left_ready, LEFT_JOBS * (c - 1) + job + 1)
                        dve.tensor_tensor(x1[:, t, :], left[job % 2][:, :], y0[:, t, :], ALU.add).then_inc(left_free, 1)
                        dve.wait_ge(left_free, LEFT_JOBS * (c - 1) + job + 1)
                        moments(0, c - 1, t, x1[:, t, :])
                        if t:
                            normalise(0, c - 1, t - 1, x1[:, t - 1, :])
                if diffuse:
                    baby_lo(c, 0, (0,))
                if attend:
                    normalise(0, c - 1, NT - 1, x1[:, NT - 1, :])
                if diffuse:
                    baby_lo(c, 0, (1, 2))
                    baby_lo(c, 1)
                if attend:
                    gather_lo(c - 1, 0)
                if diffuse:
                    y_split(c, 0, 0)
                    y_split(c, 0, 1)
                if attend:
                    leaky(c - 1, 0)
                if diffuse:
                    baby_lo(c, 2)
                if attend:
                    gather_lo(c - 1, 1)
                if diffuse:
                    y_split(c, 1, 0)
                    y_split(c, 1, 1)
                if attend:
                    leaky(c - 1, 1)
                if diffuse:
                    baby_lo(c, 3)
                    y_split(c, 2, 0)
                if attend:
                    softmax_max(c - 1)
                if diffuse:
                    y_split(c, 2, 1)
                    y_split(c, 3, 0)
                if attend:
                    softmax_sum(c - 1)
                if diffuse:
                    y_split(c, 3, 1)
                if attend:
                    for p in range(2):
                        dve.wait_ge(head_ready, 2 * (c - 1) + p + 1)
                        v = vv[:, 2 * p:2 * p + 2, :].rearrange("p b e -> p (b e)")
                        dve.tensor_tensor(v, att[p][:, :], v, ALU.mult).then_inc(av_ready, 1)
                if diffuse:
                    s_add(c, 0)
                    s_add(c, 1)
                if attend:
                    for t in range(ET):
                        dve.wait_ge(u2_hi, ET * (c - 1) + t + 1)
                        dve.tensor_tensor(ul[:, t, :], att[t][:, :], uh[:, t, :].bitcast(F32), ALU.subtract).then_inc(u2_lo, 1)
                if diffuse:
                    s_add(c, 2)
                    s_add(c, 3)
                if attend:
                    for t in range(NT):
                        dve.wait_ge(z_ready, NT * (c - 1) + t + 1)
                        dve.tensor_tensor(r2[:, t, :], att[t % 2][:, :], x1[:, t, :], ALU.add).then_inc(z_sum, 1)
                        dve.wait_ge(z_sum, NT * (c - 1) + t + 1)
                        moments(1, c - 1, t, r2[:, t, :])
                        if t:
                            normalise(1, c - 1, t - 1, r2[:, t - 1, :])
                    normalise(1, c - 1, NT - 1, r2[:, NT - 1, :])

            dve.sem_inc(tv_free, 1)
            chunks(dve, body)


_INS = ['x', 'adj', 'L0_gnn_alpha_train', 'L0_gnn_w', 'L0_gnn_d', 'L0_gnn_fc_in_w', 'L0_gnn_fc_in_b', 'L1_gnn_W_lin',
        'L1_gnn_W_val', 'L1_gnn_a', 'L1_gnn_W_out', 'L1_gnn_src', 'L1_gnn_dst']
_OUTS = [((16, 512, 128), 'float32')]


def kernel(**inputs):
    import numpy as _np
    import concourse.bacc as _bacc
    from concourse import mybir as _mybir
    from concourse.bass_utils import run_bass_kernel_spmd as _run

    nc = _bacc.Bacc("TRN2", target_bir_lowering=False, num_devices=1)
    arrays, args = {}, []
    for name in _INS:
        a = _np.ascontiguousarray(inputs[name])
        arrays[f"in_{name}_dram"] = a
        args.append(nc.dram_tensor(f"in_{name}_dram", a.shape, _mybir.dt.from_np(a.dtype), kind="ExternalInput").ap())
    for i, (shape, dtype) in enumerate(_OUTS):
        dt = _mybir.dt.from_np(_np.dtype(dtype))
        args.append(nc.dram_tensor(f"out_{i}_dram", shape, dt, kind="ExternalOutput").ap())
    graph_kernel(nc, *args)
    r = _run(nc, [arrays], core_ids=[0])
    got = tuple(r.results[0][f"out_{i}_dram"] for i in range(len(_OUTS)))
    return got[0]
```

```python
from contextlib import ExitStack
from math import comb

import concourse.bass as bass
from concourse import mybir

F32 = mybir.dt.float32
F32R = mybir.dt.float32r
I32 = mybir.dt.int32
U32 = mybir.dt.uint32
ALU = mybir.AluOpType
ACT = mybir.ActivationFunctionType

P = 128
STEPS = 8
DT = 1.0 / STEPS
LN_EPS = 1e-5
LOG_EPS = 1e-8
LRELU = 0.2
LOWEST = -3.0e38
BABY = 3


def graph_kernel(nc, x, adj, alpha, w, d, fc_w, fc_b, W_lin, W_val, a, W_out, src, dst, out):
    B, N, D = x.shape
    H, DH = a.shape
    E = src.shape[0]
    NT = N // P
    ET = E // P
    CB = 512 // D
    CHUNKS = B // CB
    W = CB * D
    BH = CB * H
    K = STEPS + 1
    assert D == P and H * DH == D and N == 512 and W == 512 and 2 * E == 512 and K == BABY * BABY
    S_JOB, OUT_JOB, LEFT_JOBS = 2 * CB, 2 * CB + NT, 2 * CB + 2 * NT
    PAIRS = NT // 2
    R_JOBS = CB * PAIRS
    SM = 8

    x_v = x.rearrange("(c b) (t p) d -> c t p b d", b=CB, p=P)
    out_v = out.rearrange("(c b) (t p) d -> c t p b d", b=CB, p=P)
    adj_v = adj.rearrange("(t p) m -> t p m", p=P)

    ctx = ExitStack()
    with ctx:
        def sb(name, shape, dt=F32):
            return ctx.enter_context(nc.sbuf_tensor(name, shape, dt))

        def sem(name):
            return ctx.enter_context(nc.semaphore(name))

        p1h, p1l = sb("p1h", [P, NT, N], F32R), sb("p1l", [P, NT, N], F32R)
        p2h, p2l = sb("p2h", [P, NT, N], F32R), sb("p2l", [P, NT, N], F32R)
        p3h, p3l = sb("p3h", [P, NT, N], F32R), sb("p3l", [P, NT, N], F32R)
        xraw = sb("xraw", [P, NT, W])
        xh, xl = sb("xh", [P, 2, NT, D], F32R), sb("xl", [P, 2, NT, D], F32R)
        kth, ktl = sb("kth", [P, 2, BABY, N], F32R), sb("ktl", [P, 2, BABY, N], F32R)
        y0, y1 = sb("y0", [P, NT, W]), sb("y1", [P, NT, W])
        y2h, y2l = sb("y2h", [P, NT, W], F32R), sb("y2l", [P, NT, W], F32R)
        sh, sl = sb("sh", [P, NT, W], F32R), sb("sl", [P, NT, W], F32R)
        x1 = sb("x1", [P, NT, W])
        rh, rl = sb("rh", [P, BABY, BABY * D], F32R), sb("rl", [P, BABY, BABY * D], F32R)
        bias = sb("bias", [P, NT, D])
        pick = sb("pick", [P, NT, 2 * E], F32R)
        onesrc = sb("onesrc", [P, ET, N], F32R)
        gh, gl = sb("gh", [P, 2, 2 * E], F32R), sb("gl", [P, 2, 2 * E], F32R)
        tv = sb("tv", [P, 2 * W * 2])
        avh, avl = sb("avh", [P, CB, E], F32R), sb("avl", [P, CB, E], F32R)
        wh, wl = sb("wh", [P, 3, D], F32R), sb("wl", [P, 3, D], F32R)
        apad = sb("apad", [P, CB * BH])
        headrow = sb("headrow", [BH, CB, D])
        logrow = sb("logrow", [BH, E])
        seg = sb("seg", [BH, E + 1])
        same = sb("same", [BH, E])
        sme, smf, smg = sb("sme", [BH, E]), sb("smf", [BH, E]), sb("smg", [BH, E])
        ident = sb("ident", [P, P])
        st = sb("st", [P, 2, NT, CB, 6])
        both, apart = sb("both", [P, 2, NT, CB]), sb("apart", [P, 2, NT, CB])
        mean = sb("mean", [P, 2, NT, CB])
        ve = sb("ve", [P, 2, NT, CB])
        nhalf = sb("nhalf", [P, 2, CB])
        rstd = sb("rstd", [P, 2, NT, CB])
        shift = sb("shift", [P, 2, NT, CB])
        small = sb("small", [P, 96])

        tt = tv[:, 0:CB * E].rearrange("p (b e) -> p b e", b=CB)
        vv = tv[:, CB * E:2 * CB * E].rearrange("p (b e) -> p b e", b=CB)
        r2 = tv[:, 0:NT * W].rearrange("p (t w) -> p t w", t=NT)
        uh, ul = gh, gl
        x1h, x1l = sh, sl

        pn = x1
        pnh, pnl = y2h, y2l
        y0f = y0[:, :, :].rearrange("p t w -> p (t w)")
        y1f = y1[:, :, :].rearrange("p t w -> p (t w)")
        qp = y0f[:, 0:K * D].rearrange("p (i e) -> p i e", i=K)
        nat = y0f[:, K * D:K * D + 5 * D].rearrange("p (i e) -> p i e", i=5)
        rf = y1f[:, 0:K * D].rearrange("p (j i e) -> p j i e", j=BABY, i=BABY)
        wt = y1f[:, K * D:K * D + D]
        wtd = y1f[:, K * D + D:K * D + 2 * D]
        edge_ops = tv
        iota_row = edge_ops[:, 0:N]
        rows_i = edge_ops[:, N:N + 2 * E].bitcast(I32)
        perm = edge_ops[:, N:N + ET * E].rearrange("p (t r) -> p t r", t=ET)
        rows_f = edge_ops[:, 2 * N:2 * N + 2 * E]
        rep = edge_ops[:, 3 * N:3 * N + 2 * ET * P].rearrange("p (s t q) -> p s t q", s=2, t=ET)
        alpha_c, exp_c, half_c, diag_c = (small[:, 4 * i:4 * i + 4] for i in range(4))
        d_c, b_c, a_c = small[:, 16:17], small[:, 17:18], small[:, 18:19]
        iota_c = small[:, 20:24]
        cols_i = small[:, 24:28].bitcast(I32)
        cols_f = small[:, 28:32]
        key_c = small[:, 32:34]
        rank_c = small[:, 34:36]
        sorted_c = small[:, 36:40].rearrange("p (t s) -> p t s", t=ET)
        idx_f = small[:, 40:42]
        idx_u = small[:, 42:44].bitcast(U32)
        a_edge = small[:, 44:46]
        log_c = small[:, 46:48]
        c_t = small[:, 48:48 + K]
        log_rep = small[:, 60:92].rearrange("p (t q) -> p t q", t=ET)
        ones = sb("ones", [P, P])
        log_eps = small[:, 92:93]
        u01 = sb("u01", [P, NT, 2])
        us_h, us_l = avh, avl
        urows = x1[0:BABY, :, :]
        crow = bias[0:BABY, :, :]

        def urow(s):
            return urows[:, s, :]

        def r_k(k):
            return rf[:, k % BABY, k // BABY, :]

        left = [ctx.enter_context(nc.psum_tensor(f"left{i}", [P, 512], F32)) for i in range(2)]
        yps = ctx.enter_context(nc.psum_tensor("yps", [P, 4, 512], F32))
        att = [ctx.enter_context(nc.psum_tensor(f"att{i}", [P, 512], F32)) for i in range(2)]

        adj_loaded, alpha_loaded, gnn_loaded = sem("adj_loaded"), sem("alpha_loaded"), sem("gnn_loaded")
        att_loaded, edges_loaded = sem("att_loaded"), sem("edges_loaded")
        ident_ready, consts = sem("ident_ready"), sem("consts")
        const_step = sem("const_step")
        dve_step = sem("dve_step")
        exp_alpha = sem("exp_alpha")
        keys_ranked = sem("keys_ranked")
        rows_sorted, rows_copied = sem("rows_sorted"), sem("rows_copied")
        idx_ready, adj_picked, logs = sem("idx_ready"), sem("adj_picked"), sem("logs")
        log_rep_ready, log_row_ready = sem("log_rep_ready"), sem("log_row_ready")
        w_turned, w_hi, wt_ready = sem("w_turned"), sem("w_hi"), sem("wt_ready")
        q_product, q_copied = sem("q_product"), sem("q_copied")
        m_ready, m_copied, r_done, r_hi, r_lo = sem("m_ready"), sem("m_copied"), sem("r_done"), sem("r_hi"), sem("r_lo")
        ones_ready = sem("ones_ready")
        half_ready, pn_scaled = sem("half_ready"), sem("pn_scaled")
        pn_ready, pn_hi, pn_lo = sem("pn_ready"), sem("pn_hi"), sem("pn_lo")
        pow_ready, pow_hi, pow_lo = sem("pow_ready"), sem("pow_hi"), sem("pow_lo")
        u_staged, u_ready, u_rows, u_turned = sem("u_staged"), sem("u_ready"), sem("u_rows"), sem("u_turned")
        u01_turned, u01_rows, c_turned = sem("u01_turned"), sem("u01_rows"), sem("c_turned")
        bias_ready = sem("bias_ready")
        x_loaded = sem("x_loaded")
        x_free = sem("x_free")
        x_slot, x_hi, x_lo = sem("x_slot"), sem("x_hi"), sem("x_lo")
        left_ready, left_free = sem("left_ready"), sem("left_free")
        left_hi = sem("left_hi")
        xt_ready, xt_hi, xt_free = sem("xt_ready"), sem("xt_hi"), sem("xt_free")
        y_ready, y_copied, y_free = sem("y_ready"), sem("y_copied"), sem("y_free")
        s_hi, s_lo = sem("s_hi"), sem("s_lo")
        ln_stats = [sem("ln1_stats"), sem("ln2_stats")]
        ln_halves = [sem("ln1_halves"), sem("ln2_halves")]
        ln_mean = [sem("ln1_mean"), sem("ln2_mean")]
        ln_var = [sem("ln1_var"), sem("ln2_var")]
        ln_rstd = [sem("ln1_rstd"), sem("ln2_rstd")]
        ln_shift = [sem("ln1_shift"), sem("ln2_shift")]
        ln_done = [sem("ln1_done"), sem("ln2_done")]
        ln_dve = [sem("ln1_dve"), sem("ln2_dve")]
        x1_hi, x1_lo = sem("x1_hi"), sem("x1_lo")
        x1_last = sem("x1_last")
        g_ready, g_hi, g_lo = sem("g_ready"), sem("g_hi"), sem("g_lo")
        lin_ready = sem("lin_ready")
        q_scaled, q_leaky, v_copied = sem("q_scaled"), sem("q_leaky"), sem("v_copied")
        score_ready, sm_step, sm_exp = sem("score_ready"), sem("sm_step"), sem("sm_exp")
        head_ready, av_ready, av_hi, av_lo = sem("head_ready"), sem("av_ready"), sem("av_hi"), sem("av_lo")
        u2_ready, u2_hi, u2_lo = sem("u2_ready"), sem("u2_hi"), sem("u2_lo")
        z_ready, z_sum = sem("z_ready"), sem("z_sum")
        stored = sem("stored")
        tv_free = sem("tv_free")

        def need(eng, s, value):
            if not isinstance(value, int) or value > 0:
                eng.wait_ge(s, value)

        def xt_bank(b):
            return att[(0, 1, 1, 1)[b]]

        DVE_TILES = (1, 0)
        LAST_DVE_TILES = 2

        def passes(h1, l1, h2, l2):
            return ((h1, h2), (h1, l2), (l1, h2))

        def chunks(eng, body, tail):
            body(0, False)
            with eng.Fori(1, CHUNKS) as c:
                body(c, True)
            tail(CHUNKS - 1)

        block = ctx.enter_context(nc.Block())

        @block.sync
        def _(sp):
            def load_x(c):
                for t in range(NT):
                    sp.dma_start(xraw[:, t, :].rearrange("p (b d) -> p b d", b=CB), x_v[c, t]).then_inc(x_loaded, 16)

            def reload_x(c):
                sp.wait_ge(xt_ready, CB * c)
                sp.sem_inc(x_free, 1)
                sp.wait_ge(x_lo, CB * c)
                sp.sem_inc(x_free, 1)
                load_x(c)

            def store(cc, last=False):
                for t in range(NT):
                    own = t - (NT - LAST_DVE_TILES)
                    if last and own >= 0:
                        sp.wait_ge(ln_dve[1], own + 1)
                    else:
                        sp.wait_ge(ln_done[1], NT * cc + t + 1)
                    sp.dma_start(out_v[cc, t], r2[:, t, :].rearrange("p (b d) -> p b d", b=CB)).then_inc(stored, 16)
                sp.wait_ge(stored, 16 * NT * (cc + 1))
                sp.sem_inc(tv_free, 1)

            for t in range(NT):
                sp.dma_start(pn[:, t, :], adj_v[t]).then_inc(adj_loaded, 16)
            load_x(0)
            for s, e in enumerate((src, dst)):
                sp.dma_start(rows_i[:, s * E:(s + 1) * E], e.rearrange("(o e) -> o e", o=1).broadcast_to([P, E])).then_inc(edges_loaded, 16)
                sp.dma_start(cols_i[:, 2 * s:2 * s + 2], e.rearrange("(t p) -> p t", p=P),
                             allow_slow_non_contiguous=True).then_inc(edges_loaded, 16)
            for i, m in enumerate((W_lin, W_val, W_out)):
                sp.dma_start(nat[:, 2 + i, :], m).then_inc(att_loaded, 16)
            sp.dma_start(a_c, a.rearrange("h (e o) -> (h e) o", o=1)).then_inc(att_loaded, 16)

            reload_x(1)
            with sp.Fori(1, CHUNKS - 1) as c:
                reload_x(c + 1)
                store(c - 1)
            store(CHUNKS - 2)
            store(CHUNKS - 1, True)

        @block.gpsimd
        def _(pool):
            pool.memset(ident[:, :], 0.0).then_inc(const_step, 1)
            pool.wait_ge(const_step, 1)
            pool.affine_select(out=ident[:, :], in_=ident[:, :], compare_op=ALU.not_equal, fill=1.0,
                               base=0, pattern=[[-1, P]], channel_multiplier=1).then_inc(ident_ready, 1)
            pool.memset(headrow[:, :, :], 1.0).then_inc(const_step, 1)
            pool.iota(iota_row, pattern=[[1, N]], base=0, channel_multiplier=0,
                      allow_small_or_imprecise_dtypes=True).then_inc(consts, 1)
            pool.iota(iota_c, pattern=[[P, NT]], base=0, channel_multiplier=1,
                      allow_small_or_imprecise_dtypes=True).then_inc(consts, 1)
            pool.wait_ge(const_step, 2)
            heads = headrow[:, :, :].rearrange("q b (h e) -> q b h e", h=H)
            pool.affine_select(out=heads, in_=heads, compare_op=ALU.is_equal, fill=0.0,
                               base=0, pattern=[[-H, CB], [-1, H], [0, DH]], channel_multiplier=1).then_inc(consts, 1)
            pool.memset(nhalf[:, :, :], -0.5).then_inc(consts, 1)

            def split_x(c, b):
                if b >= 2 or not isinstance(c, int):
                    pool.wait_ge(left_ready, LEFT_JOBS * c + 2 * (b - 1) if b >= 2 else LEFT_JOBS * (c - 1) + 2 * (b + 3))
                pool.sem_inc(x_slot, 1)
                pool.tensor_copy(xh[:, b % 2, :, :], xraw[:, :, b * D:(b + 1) * D]).then_inc(x_hi, 1)
                pool.wait_ge(x_hi, CB * c + b + 1)
                pool.tensor_tensor(xl[:, b % 2, :, :], xraw[:, :, b * D:(b + 1) * D],
                                   xh[:, b % 2, :, :].bitcast(F32), ALU.subtract).then_inc(x_lo, 1)

            def rsqrt(k, cc, t, n):
                ts = slice(t, t + n)
                pool.wait_ge(ln_var[k], NT * cc + t + n)
                pool.tensor_tensor(rstd[:, k, ts, :], ve[:, k, ts, :], nhalf[:, 0:n, :], ALU.pow).then_inc(ln_rstd[k], n)
                pool.wait_ge(ln_rstd[k], NT * cc + t + n)
                pool.tensor_tensor(shift[:, k, ts, :], mean[:, k, ts, :], rstd[:, k, ts, :], ALU.mult).then_inc(ln_shift[k], n)

            def body(c, attend):
                head = not attend
                pool.wait_ge(x_loaded, 16 * NT * (c + 1))
                split_x(c, 0)
                if head:
                    for t in (1, 3):
                        pool.wait_ge(pn_hi, t + 1)
                        pool.tensor_tensor(pnl[:, t, :], pn[:, t, :], pnh[:, t, :].bitcast(F32), ALU.subtract).then_inc(pn_lo, 1)
                else:
                    rsqrt(0, c - 1, 0, 2)
                split_x(c, 1)
                if attend:
                    rsqrt(0, c - 1, 2, 2)
                split_x(c, 2)
                if head:
                    pool.wait_ge(idx_ready, 1)
                    adj_flat = adj.rearrange("n (m o) -> (n m) o", o=1)
                    for t in range(ET):
                        pool.indirect_dma_start(a_edge[:, t:t + 1], None, adj_flat,
                                                bass.IndirectOffsetOnAxis(ap=idx_u[:, t:t + 1], axis=0)).then_inc(adj_picked, 16)
                split_x(c, 3)
                if attend:
                    for p in range(2):
                        pool.wait_ge(av_hi, 2 * (c - 1) + p + 1)
                        pool.tensor_tensor(avl[:, 2 * p:2 * p + 2, :], vv[:, 2 * p:2 * p + 2, :],
                                           avh[:, 2 * p:2 * p + 2, :].bitcast(F32), ALU.subtract).then_inc(av_lo, 1)
                    rsqrt(1, c - 1, 0, 2)
                    rsqrt(1, c - 1, 2, 2)

            def x1_split(cc, t):
                pool.wait_ge(x1_hi, NT * cc + t + 1)
                pool.tensor_tensor(y2l[:, t, :], x1[:, t, :], y2h[:, t, :].bitcast(F32), ALU.subtract).then_inc(x1_lo, 1)

            def tail(cc):
                rsqrt(0, cc, 0, 1)
                rsqrt(0, cc, 1, 1)
                rsqrt(0, cc, 2, 1)
                x1_split(cc, 0)
                rsqrt(0, cc, 3, 1)
                x1_split(cc, 1)
                for t in range(NT):
                    rsqrt(1, cc, t, 1)

            chunks(pool, body, tail)

        @block.scalar
        def _(act):
            col = "(p o) -> p o"
            act.dma_start(alpha_c, alpha.rearrange("(t p) -> p t", p=P), allow_slow_non_contiguous=True).then_inc(alpha_loaded, 16)
            act.dma_start(nat[:, 0, :], w).then_inc(gnn_loaded, 16)
            act.dma_start(nat[:, 1, :], fc_w).then_inc(gnn_loaded, 16)
            act.dma_start(d_c, d.rearrange(col, o=1)).then_inc(gnn_loaded, 16)
            act.dma_start(b_c, fc_b.rearrange(col, o=1)).then_inc(gnn_loaded, 16)
            act.wait_ge(ones_ready, 1)
            act.activation(small[:, 93:94], ones[:, 0:1], ACT.Exp)
            act.wait_ge(alpha_loaded, 16)
            act.activation(exp_c, alpha_c, ACT.Exp, scale=-1.0).then_inc(exp_alpha, 1)
            act.wait_ge(adj_loaded, 16 * NT)
            act.wait_ge(half_ready, 1)
            for t in range(PAIRS, NT):
                act.activation(pn[:, t, :], pn[:, t, :], ACT.Copy, scale=half_c[:, t:t + 1]).then_inc(pn_scaled, 1)
            for t in range(NT):
                act.wait_ge(pn_ready, t + 1)
                act.activation(pnh[:, t, :], pn[:, t, :], ACT.Copy).then_inc(pn_hi, 1)
            def power_hi(n, ph):
                for t in range(NT):
                    act.wait_ge(pow_ready, NT * n + t + 1)
                    act.activation(ph[:, t, :], yps[:, t, :], ACT.Copy).then_inc(pow_hi, 1)

            def xt_copy(c, b):
                need(act, y_ready, R_JOBS * c + PAIRS * (b - 1))
                act.wait_ge(xt_ready, CB * c + b + 1)
                act.activation(kth[:, b % 2, 0, :], xt_bank(b)[:, :], ACT.Copy).then_inc(xt_hi, 1)

            def baby_hi(c, b, j):
                act.wait_ge(left_ready, LEFT_JOBS * c + 2 * b + j)
                act.activation(kth[:, b % 2, j, :], left[(j - 1) % 2][:, :], ACT.Copy).then_inc(left_hi, 1)

            def normalise(k, cc, t, tiles):
                act.wait_ge(ln_shift[k], NT * cc + t + 1)
                for b in range(CB):
                    r = tiles[:, t, b * D:(b + 1) * D]
                    ins = act.activation(r, r, ACT.Identity, bias=shift[:, k, t, b:b + 1], scale=rstd[:, k, t, b:b + 1])
                ins.then_inc(ln_done[k], 1)

            def x1_copy(cc, t, hi=x1h, dve_tiles=DVE_TILES[0]):
                own = t - (NT - dve_tiles)
                if own < 0:
                    act.wait_ge(ln_done[0], (NT - DVE_TILES[0]) * cc + t + 1)
                else:
                    act.wait_ge(ln_dve[0], DVE_TILES[0] * cc + own + 1)
                act.activation(hi[:, t, :], x1[:, t, :], ACT.Copy).then_inc(x1_hi, 1)

            def y_copy(c, b, p):
                act.wait_ge(y_ready, R_JOBS * c + PAIRS * b + p + 1)
                ps = yps[:, 2 * p:2 * p + 2, :]
                act.activation(y2h[:, 2 * p:2 * p + 2, b * D:(b + 1) * D], ps[:, :, 2 * D:3 * D], ACT.Copy)
                act.activation(y1[:, 2 * p:2 * p + 2, b * D:(b + 1) * D], ps[:, :, D:2 * D], ACT.Copy).then_inc(y_copied, 1)

            def gather_hi(cc, b, bank, slot):
                act.wait_ge(g_ready, CB * cc + b + 1)
                act.activation(slot, bank, ACT.Copy).then_inc(g_hi, 1)

            def lin(cc, p, q_bank, v_bank):
                if p == 0:
                    act.wait_ge(tv_free, cc + 1)
                act.wait_ge(lin_ready, 4 * cc + 2 * p + 1)
                act.activation(tt[:, 2 * p:2 * p + 2, :], q_bank[:, :].rearrange("p (b e) -> p b e", b=2),
                               ACT.Copy, scale=LRELU).then_inc(q_scaled, 1)
                act.wait_ge(lin_ready, 4 * cc + 2 * p + 2)
                act.activation(vv[:, 2 * p:2 * p + 2, :], v_bank[:, :].rearrange("p (b e) -> p b e", b=2),
                               ACT.Copy).then_inc(v_copied, 1)

            def exponential(cc):
                act.wait_ge(sm_step, SM * cc + 4)
                act.activation(smf[:, :], smg[:, :], ACT.Exp).then_inc(sm_exp, 1)

            def av_copy(cc, p):
                act.wait_ge(av_ready, 2 * cc + p + 1)
                act.activation(avh[:, 2 * p:2 * p + 2, :], vv[:, 2 * p:2 * p + 2, :], ACT.Copy).then_inc(av_hi, 1)

            def u_hi(cc, t):
                act.wait_ge(u2_ready, ET * cc + t + 1)
                act.activation(uh[:, t, :], att[t][:, :], ACT.Copy).then_inc(u2_hi, 1)

            def body(c, attend):
                head = not attend
                if head:
                    power_hi(0, p1h)
                    act.wait_ge(q_product, 1)
                    act.activation(qp[:, 1, :], att[0][:, 2 * D:3 * D], ACT.Copy, scale=DT).then_inc(q_copied, 1)
                    act.wait_ge(q_product, 2)
                    act.activation(qp[:, 2, :], att[0][:, 3 * D:4 * D], ACT.Copy).then_inc(q_copied, 1)
                    baby_hi(c, 0, 1)
                    act.wait_ge(q_product, 3)
                    act.activation(qp[:, 3:5, :].rearrange("p i e -> p (i e)"), att[1][:, 0:2 * D], ACT.Copy).then_inc(q_copied, 1)
                    power_hi(1, p2h)
                    act.wait_ge(q_product, 4)
                    act.activation(qp[:, 5:9, :].rearrange("p i e -> p (i e)"), att[0][:, :], ACT.Copy).then_inc(q_copied, 1)
                    baby_hi(c, 0, 2)
                    power_hi(2, p3h)
                    act.wait_ge(r_done, 1)
                    act.activation(rh[:, :, :], rf[:, :, :, :].rearrange("p j i e -> p j (i e)"), ACT.Copy).then_inc(r_hi, 1)
                xt_copy(c, 0)
                if head:
                    xt_copy(c, 1)
                else:
                    act.wait_ge(left_ready, LEFT_JOBS * c)
                    normalise(0, c - 1, 0, x1)
                    x1_copy(c - 1, 0)
                    baby_hi(c, 0, 1)
                    normalise(0, c - 1, 1, x1)
                    x1_copy(c - 1, 1)
                    baby_hi(c, 0, 2)
                    xt_copy(c, 1)
                    normalise(0, c - 1, 2, x1)
                    x1_copy(c - 1, 2)
                    x1_copy(c - 1, 3)
                baby_hi(c, 1, 1)
                baby_hi(c, 1, 2)
                if head:
                    act.wait_ge(w_turned, 2)
                    act.activation(wh[:, :, :].rearrange("p i e -> p (i e)"), att[0][:, 0:3 * D], ACT.Copy).then_inc(w_hi, 1)
                if attend:
                    gather_hi(c - 1, 0, att[0][:, :], gh[:, 0, :])
                    gather_hi(c - 1, 1, att[1][:, :], gh[:, 1, :])
                y_copy(c, 0, 0)
                y_copy(c, 0, 1)
                if attend:
                    lin(c - 1, 0, *att)
                baby_hi(c, 2, 1)
                xt_copy(c, 2)
                if attend:
                    gather_hi(c - 1, 2, att[0][:, :], gh[:, 0, :])
                    gather_hi(c - 1, 3, att[1][:, :], gh[:, 1, :])
                baby_hi(c, 2, 2)
                if attend:
                    lin(c - 1, 1, *att)
                y_copy(c, 1, 0)
                if attend:
                    exponential(c - 1)
                y_copy(c, 1, 1)
                xt_copy(c, 3)
                baby_hi(c, 3, 1)
                baby_hi(c, 3, 2)
                if head:
                    act.wait_ge(adj_picked, 16 * ET)
                    act.activation(log_c, a_edge, ACT.Ln, bias=log_eps).then_inc(logs, 1)
                if attend:
                    for p in range(2):
                        av_copy(c - 1, p)
                y_copy(c, 2, 0)
                y_copy(c, 2, 1)
                if attend:
                    for t in range(ET):
                        u_hi(c - 1, t)
                y_copy(c, 3, 0)
                y_copy(c, 3, 1)
                for t in range(NT):
                    act.wait_ge(left_free, LEFT_JOBS * c + S_JOB + t + 1)
                    act.activation(sh[:, t, :], y1[:, t, :], ACT.Copy).then_inc(s_hi, 1)
                if attend:
                    for t in range(NT):
                        normalise(1, c - 1, t, r2)

            def tail(cc):
                for t in range(NT):
                    if t < NT - LAST_DVE_TILES:
                        normalise(0, cc, t, x1)
                    x1_copy(cc, t, y2h, LAST_DVE_TILES)
                for b in range(CB):
                    gather_hi(cc, b, yps[:, b, :], (gh[:, b, :] if b < 2 else kth[:, 0, b - 2, :]))
                lin(cc, 0, *att)
                lin(cc, 1, *left)
                exponential(cc)
                for p in range(2):
                    av_copy(cc, p)
                for t in range(ET):
                    u_hi(cc, t)
                for t in range(NT - LAST_DVE_TILES):
                    normalise(1, cc, t, r2)

            chunks(act, body, tail)

        @block.tensor
        def _(pe):
            def flat(ap):
                return ap.rearrange("p i e -> p (i e)")

            def accumulate(out_ap, todo):
                for i, (l, r) in enumerate(todo):
                    mm = pe.matmul(out_ap, l, r, start=(i == 0), stop=(i == len(todo) - 1))
                return mm

            pe.wait_ge(ident_ready, 1)
            pe.wait_ge(gnn_loaded, 64)
            for i in range(2):
                mm = pe.transpose(att[0][:, i * D:(i + 1) * D], nat[:, i, :], ident[:, :])
            mm.then_inc(w_turned, 1)
            pe.wait_ge(pn_ready, NT)
            for t in range(NT):
                for n in range(NT):
                    mm = pe.transpose(yps[:, t, n * P:(n + 1) * P], pn[:, n, t * P:(t + 1) * P], ident[:, :])
                mm.then_inc(pow_ready, 1)
            pe.wait_ge(wt_ready, 1)
            pe.matmul(att[0][:, 2 * D:3 * D], wtd, wt, start=True, stop=True).then_inc(q_product, 1)
            pe.wait_ge(q_copied, 1)
            pe.matmul(att[0][:, 3 * D:4 * D], qp[:, 1, :], qp[:, 1, :], start=True, stop=True).then_inc(q_product, 1)

            def power(n, ph, pl):
                pe.wait_ge(pow_lo, NT * (n - 1))
                for t in range(NT):
                    cols = slice(t * P, (t + 1) * P)
                    accumulate(yps[:, t, :], [q for k in range(NT) for q in passes(
                        pnh[:, k, cols], pnl[:, k, cols], ph[:, k, :], pl[:, k, :])]).then_inc(pow_ready, 1)

            def u_step(s, ph, pl):
                pe.wait_ge(u_staged, s + 1)
                accumulate(att[1][:, :], [q for m in range(NT) for q in passes(
                    us_h[:, m, 0:P], us_l[:, m, 0:P], ph[:, m, :], pl[:, m, :])]).then_inc(u_ready, 1)

            def turn(s, n):
                pe.wait_ge(u_rows, s + 1)
                for t in range(NT):
                    mm = pe.matmul(att[0][:, n * t:n * t + n], urow(s)[0:n, t * P:(t + 1) * P], ident[0:n, 0:n], start=True, stop=True)
                mm.then_inc(u_turned, 1)

            def left_bank(c, job):
                need(pe, left_free, LEFT_JOBS * c + job - 1)
                return left[job % 2]

            def turn_x(c, b):
                for t in range(NT):
                    mm = pe.transpose(xt_bank(b)[:, t * P:(t + 1) * P], xraw[:, t, b * D:(b + 1) * D], ident[:, :])
                mm.then_inc(xt_ready, 1)

            def baby(c, b, j, ph, pl):
                pe.wait_ge(x_lo, CB * c + b + 1)
                accumulate(left_bank(c, 2 * b + j - 1)[:, :], [q for m in range(NT) for q in passes(
                    xh[:, b % 2, m, :], xl[:, b % 2, m, :], ph[:, m, :], pl[:, m, :])]).then_inc(left_ready, 1)

            def rights(c, b, p):
                if p == 0:
                    pe.wait_ge(xt_free, CB * c + b + 1)
                    pe.wait_ge(left_free, LEFT_JOBS * c + 2 * (b + 1))
                need(pe, y_free, R_JOBS * c + PAIRS * b + p - 1)
                for n in (2 * p, 2 * p + 1):
                    cols = slice(n * P, (n + 1) * P)
                    mm = accumulate(yps[:, n, 0:BABY * D], [q for j in range(BABY) for q in passes(
                        kth[:, b % 2, j, cols], ktl[:, b % 2, j, cols], rh[:, j, :], rl[:, j, :])])
                mm.then_inc(y_ready, 1)

            def giant(c, job, n, zh, zl, arrived, count):
                ps = left_bank(c, job)
                cols = slice(n * P, (n + 1) * P)
                for m in range(NT):
                    if n == 0 and count(m) is not None:
                        pe.wait_ge(arrived, count(m))
                    for i, (l, r) in enumerate(passes(p3h[:, m, cols], p3l[:, m, cols], zh[:, m, :], zl[:, m, :])):
                        mm = pe.matmul(ps[:, :], l, r, start=(m == 0 and i == 0), stop=(m == NT - 1 and i == 2))
                mm.then_inc(left_ready, 1)

            def gather(cc, b):
                cols = slice(b * D, (b + 1) * D)
                accumulate(att[b % 2][:, :], [(x[:, t, cols], pick[:, t, :]) for t in range(NT) for x in (x1h, x1l)]).then_inc(g_ready, 1)

            def lin(cc, p, hi, lo, banks):
                pe.wait_ge(g_lo, CB * cc + 2 * p + 2)
                for i in range(2):
                    cols = slice(i * E, (i + 1) * E)
                    accumulate(banks[i][:, :].rearrange("p (b e) -> p b e", b=2),
                               passes(wh[:, i, :], wl[:, i, :], hi[:, 0:2, cols], lo[:, 0:2, cols])).then_inc(lin_ready, 1)

            def scores(cc, bank):
                pe.wait_ge(q_leaky, 2 * (cc + 1))
                accumulate(bank, [(apad[:, b * BH:(b + 1) * BH], tt[:, b, :]) for b in range(CB)]).then_inc(score_ready, 1)

            def attention(cc, *banks):
                pe.wait_ge(sm_step, SM * (cc + 1))
                pe.wait_ge(v_copied, 2 * (cc + 1))
                for p in range(2):
                    for b in (2 * p, 2 * p + 1):
                        mm = pe.matmul(banks[p][:, (b % 2) * E:(b % 2 + 1) * E], headrow[:, b, :], sme[:, :], start=True, stop=True)
                    mm.then_inc(head_ready, 1)

            def u_tiles(cc):
                pe.wait_ge(av_lo, 2 * (cc + 1))
                for t in range(ET):
                    es = slice(t * P, (t + 1) * P)
                    for b in range(CB):
                        mm = accumulate(att[t][:, b * D:(b + 1) * D], passes(avh[:, b, es], avl[:, b, es], wh[:, 2, :], wl[:, 2, :]))
                    mm.then_inc(u2_ready, 1)

            def z_sums(cc, n, bank):
                if n == 0:
                    pe.wait_ge(u2_lo, ET * (cc + 1))
                cols = slice(n * P, (n + 1) * P)
                accumulate(bank, [(onesrc[:, t, cols], u[:, t, :]) for t in range(ET) for u in (uh, ul)]).then_inc(z_ready, 1)

            def s_tile(c, t):
                giant(c, S_JOB + t, t, y2h, y2l, y_free, lambda m: R_JOBS * c + R_JOBS - 1 + m // 2 if m % 2 == 0 else None)

            def out_tile(c, t):
                giant(c, OUT_JOB + t, t, sh, sl, s_lo, lambda m: NT * c + m + 1)

            def body(c, attend):
                head = not attend
                if attend:
                    out_tile(c - 1, 0)
                    pe.wait_ge(x_loaded, 16 * NT * (c + 1))
                    pe.wait_ge(z_sum, NT * (c - 1) + 3)
                    turn_x(c, 0)
                if attend:
                    out_tile(c - 1, 1)
                    out_tile(c - 1, 2)
                    out_tile(c - 1, 3)
                if head:
                    pe.wait_ge(pow_lo, NT)
                    baby(c, 0, 1, p1h, p1l)
                    pe.wait_ge(q_copied, 2)
                    pe.matmul(att[1][:, 0:2 * D], qp[:, 2, :], flat(qp[:, 1:3, :]), start=True, stop=True).then_inc(q_product, 1)
                    pe.wait_ge(pn_lo, NT)
                    power(2, p1h, p1l)
                    pe.wait_ge(q_copied, 3)
                    pe.matmul(att[0][:, :], qp[:, 4, :], flat(qp[:, 1:5, :]), start=True, stop=True).then_inc(q_product, 1)
                    pe.wait_ge(pow_lo, 2 * NT)
                    baby(c, 0, 2, p2h, p2l)
                    pe.wait_ge(q_copied, 4)
                    pe.matmul(att[1][:, :], nat[:, 1, :], flat(qp[:, 1:5, :]), start=True, stop=True)
                    mm = pe.matmul(att[0][:, :], nat[:, 1, :], flat(qp[:, 5:9, :]), start=True, stop=True)
                    mm.then_inc(m_ready, 1)
                    power(3, p2h, p2l)
                    pe.wait_ge(m_copied, 1)
                    turn_x(c, 0)
                    turn_x(c, 1)
                else:
                    pe.wait_ge(z_sum, NT * c)
                    turn_x(c, 1)
                    baby(c, 0, 1, p1h, p1l)
                    baby(c, 0, 2, p2h, p2l)
                baby(c, 1, 1, p1h, p1l)
                baby(c, 1, 2, p2h, p2l)
                if head:
                    pe.wait_ge(xt_free, 1)
                    pe.wait_ge(att_loaded, 64)
                    for i in range(3):
                        pe.transpose(att[0][:, i * D:(i + 1) * D], nat[:, 2 + i, :], ident[:, :])
                    pe.wait_ge(keys_ranked, 1)
                    for r in range(ET):
                        accumulate(att[0][:, 3 * D + 2 * r:3 * D + 2 * r + 2],
                                   [(perm[:, t, r * P:(r + 1) * P], cols_f[:, t::2]) for t in range(ET)])
                    for i in range(K):
                        col = 3 * D + 2 * ET + i
                        mm = pe.matmul(att[0][:, col:col + 1], qp[:, i, :], b_c, start=True, stop=True)
                    mm.then_inc(w_turned, 1)
                    pe.wait_ge(xt_free, 2)
                    for s in range(2):
                        mm = accumulate(att[1][:, s * E:(s + 1) * E], [(rep[:, s, t, :], perm[:, t, :]) for t in range(ET)])
                    mm.then_inc(rows_sorted, 1)
                    pe.wait_ge(r_lo, 1)
                    pe.wait_ge(pow_lo, 3 * NT)
                if attend:
                    pe.wait_ge(xt_free, CB * c + 2)
                    pe.wait_ge(x1_lo, NT * c)
                    gather(c - 1, 0)
                    gather(c - 1, 1)
                rights(c, 0, 0)
                rights(c, 0, 1)
                if head:
                    pe.wait_ge(rows_copied, 1)
                    for t in range(NT):
                        mm = pe.matmul(att[1][0:2, t * P:(t + 1) * P], u01[:, t, :], ident[:, :], start=True, stop=True)
                    mm.then_inc(u01_turned, 1)
                if attend:
                    lin(c - 1, 0, gh, gl, att)
                baby(c, 2, 1, p1h, p1l)
                if head:
                    pe.wait_ge(u01_rows, 1)
                else:
                    pe.wait_ge(v_copied, 2 * c - 1)
                    pe.wait_ge(q_leaky, 2 * c - 1)
                turn_x(c, 2)
                if attend:
                    gather(c - 1, 2)
                    pe.wait_ge(xt_free, CB * c + 3)
                    gather(c - 1, 3)
                baby(c, 2, 2, p2h, p2l)
                if attend:
                    lin(c - 1, 1, gh, gl, att)
                rights(c, 1, 0)
                if head:
                    pe.wait_ge(xt_free, 3)
                    u_step(0, p1h, p1l)
                    for i in range(BABY):
                        pe.matmul(att[0][0:BABY, i * P:(i + 1) * P], c_t[:, BABY * i:BABY * i + BABY], ident[:, :], start=True, stop=True)
                    mm = pe.matmul(att[0][0:1, 3 * P:4 * P], c_t[:, 2:3], ident[:, :], start=True, stop=True)
                    mm.then_inc(c_turned, 1)
                if attend:
                    scores(c - 1, att[0][0:BH, 0:E])
                rights(c, 1, 1)
                if head:
                    turn(0, 1)
                else:
                    pe.wait_ge(v_copied, 2 * c)
                turn_x(c, 3)
                baby(c, 3, 1, p1h, p1l)
                baby(c, 3, 2, p2h, p2l)
                pe.wait_ge(xt_free, CB * (c + 1))
                if head:
                    u_step(1, p3h, p3l)
                else:
                    attention(c - 1, *att)
                rights(c, 2, 0)
                rights(c, 2, 1)
                if head:
                    turn(1, BABY)
                else:
                    u_tiles(c - 1)
                rights(c, 3, 0)
                rights(c, 3, 1)
                if head:
                    u_step(2, p3h, p3l)
                else:
                    z_sums(c - 1, 0, att[0][:, :])
                    z_sums(c - 1, 1, att[1][:, :])
                s_tile(c, 0)
                s_tile(c, 1)
                if head:
                    pe.wait_ge(log_rep_ready, 1)
                    for i in range(ET):
                        mm = pe.matmul(att[0][0:BH, i * P:(i + 1) * P], log_rep[:, i, :], ident[:, :], start=True, stop=True)
                    mm.then_inc(log_row_ready, 1)
                s_tile(c, 2)
                if attend:
                    pe.wait_ge(z_sum, NT * c + 1)
                    z_sums(c - 1, 2, att[0][:, :])
                s_tile(c, 3)
                if attend:
                    pe.wait_ge(z_sum, NT * c + 2)
                    z_sums(c - 1, 3, att[1][:, :])
                if head:
                    pe.wait_ge(u_rows, 3)
                    for t in range(NT):
                        cols = slice(t * P, (t + 1) * P)
                        mm = accumulate(att[1][:, cols], [(urow(s)[0:n, cols], crow[0:n, i, :])
                                                          for s, n, i in ((3, 2, 0), (0, 1, 3), (1, BABY, 1), (2, BABY, 2))])
                    mm.then_inc(bias_ready, 1)

            def tail(cc):
                for t in range(NT):
                    out_tile(cc, t)
                for t in range(NT):
                    if t < NT - LAST_DVE_TILES:
                        pe.wait_ge(x1_lo, NT * cc + t + 1)
                    else:
                        pe.wait_ge(x1_last, t - (NT - LAST_DVE_TILES) + 1)
                    for b in range(CB):
                        cols = slice(b * D, (b + 1) * D)
                        pe.matmul(yps[:, b, :], y2h[:, t, cols], pick[:, t, :], start=(t == 0), stop=False)
                        mm = pe.matmul(yps[:, b, :], y2l[:, t, cols], pick[:, t, :], start=False, stop=(t == NT - 1))
                        if t == NT - 1:
                            mm.then_inc(g_ready, 1)
                pe.wait_ge(z_sum, NT * (cc + 1))
                lin(cc, 0, gh, gl, att)
                pe.wait_ge(left_free, LEFT_JOBS * (cc + 1))
                lin(cc, 1, kth[:, 0, :, :], ktl[:, 0, :, :], left)
                scores(cc, yps[0:BH, 0, 0:E])
                attention(cc, yps[:, 1, :], yps[:, 2, :])
                u_tiles(cc)
                for n in range(NT):
                    z_sums(cc, n, yps[:, n, :])

            chunks(pe, body, tail)

        @block.vector
        def _(dve):
            done = [0]

            def link(ins):
                done[0] += 1
                ins.then_inc(dve_step, 1)
                dve.wait_ge(dve_step, done[0])

            dve.memset(ones[:, :], 1.0).then_inc(ones_ready, 1)
            dve.memset(us_h[:, :, :].rearrange("p t c -> p (t c)").bitcast(F32), 0.0)
            dve.memset(us_l[:, :, :].rearrange("p t c -> p (t c)").bitcast(F32), 0.0)
            dve.memset(apad[:, :], 0.0)
            dve.memset(seg[:, :], LOWEST)
            dve.memset(same[:, :], 0.0)
            dve.memset(u01[:, :, 0:1], 1.0)
            dve.memset(log_eps, LOG_EPS).then_inc(consts, 1)
            dve.wait_ge(exp_alpha, 1)
            link(dve.tensor_scalar(exp_c, exp_c, 1.0, None, ALU.add))
            link(dve.reciprocal(half_c, exp_c))
            link(dve.tensor_scalar(half_c, half_c, DT / 2, None, ALU.mult))
            dve.sem_inc(half_ready, 1)
            link(dve.tensor_scalar(diag_c, half_c, -1.0, 1.0 - DT, ALU.mult, ALU.add))
            dve.wait_ge(adj_loaded, 16 * NT)
            for t in range(PAIRS):
                ins = dve.tensor_scalar(pn[:, t, :], pn[:, t, :], half_c[:, t:t + 1], None, ALU.mult)
            link(ins)
            dve.wait_ge(ident_ready, 1)
            for t in range(NT):
                if t >= PAIRS:
                    dve.wait_ge(pn_scaled, t - PAIRS + 1)
                dg = pn[:, t, t * P:(t + 1) * P]
                dve.scalar_tensor_tensor(out=dg, in0=ident[:, :], scalar=diag_c[:, t:t + 1], in1=dg,
                                         op0=ALU.mult, op1=ALU.add).then_inc(pn_ready, 1)
            dve.wait_ge(gnn_loaded, 64)
            dve.wait_ge(w_turned, 1)
            dve.tensor_scalar(d_c, d_c, 0.0, 1.0, ALU.max, ALU.min)
            link(dve.tensor_copy(wt, att[0][:, 0:D]))
            dve.tensor_scalar(wtd, wt, d_c, None, ALU.mult)
            dve.tensor_copy(r_k(STEPS), att[0][:, D:2 * D]).then_inc(wt_ready, 1)
            dve.tensor_copy(qp[:, 0, :], ident[:, :])

            def power_lo(n, ph, pl):
                for t in range(NT):
                    dve.wait_ge(pow_hi, NT * n + t + 1)
                    dve.tensor_tensor(pl[:, t, :], yps[:, t, :], ph[:, t, :].bitcast(F32), ALU.subtract).then_inc(pow_lo, 1)

            def rank_edges():
                dve.wait_ge(edges_loaded, 64)
                dve.wait_ge(consts, 5)
                dve.tensor_copy(rows_f, rows_i)
                link(dve.tensor_copy(cols_f, cols_i))
                dve.scalar_tensor_tensor(out=rows_f[:, 0:E], in0=rows_f[:, 0:E], scalar=float(E), in1=iota_row[:, 0:E], op0=ALU.mult, op1=ALU.add)
                dve.scalar_tensor_tensor(out=key_c, in0=cols_f[:, 0:2], scalar=float(E), in1=iota_c[:, 0:2], op0=ALU.mult, op1=ALU.add)
                for s in range(2):
                    for t in range(ET):
                        ins = dve.tensor_scalar(rep[:, s, t, :], ones[:, :], cols_f[:, 2 * s + t:2 * s + t + 1], None, ALU.mult)
                link(ins)
                for t in range(ET):
                    link(dve.tensor_scalar(rows_f[:, E:2 * E], rows_f[:, 0:E], key_c[:, t:t + 1], 0.0, ALU.is_lt, ALU.add,
                                           accum_out=rank_c[:, t:t + 1]))
                for t in range(ET):
                    ins = dve.tensor_scalar(perm[:, t, :], iota_row[:, 0:E], rank_c[:, t:t + 1], None, ALU.is_equal)
                ins.then_inc(keys_ranked, 1)

            def edge_index():
                dve.wait_ge(w_hi, 1)
                dve.tensor_tensor(wl[:, :, :].rearrange("p i e -> p (i e)"), att[0][:, 0:3 * D],
                                  wh[:, :, :].rearrange("p i e -> p (i e)").bitcast(F32), ALU.subtract)
                for k in range(K):
                    col = 3 * D + 2 * ET + STEPS - k
                    dve.tensor_scalar(c_t[:, k:k + 1], att[0][:, col:col + 1], float(comb(STEPS, k)), None, ALU.mult)
                link(dve.tensor_copy(sorted_c, att[0][:, 3 * D:3 * D + 2 * ET].rearrange("p (t s) -> p t s", t=ET)))
                link(dve.scalar_tensor_tensor(out=idx_f, in0=sorted_c[:, :, 0], scalar=float(N), in1=sorted_c[:, :, 1],
                                              op0=ALU.mult, op1=ALU.add))
                dve.tensor_copy(idx_u, idx_f).then_inc(idx_ready, 1)
                dve.wait_ge(rows_sorted, 1)
                link(dve.tensor_copy(rows_f, att[1][:, :]))
                dve.sem_inc(rows_copied, 1)

            def edge_onehots():
                link(dve.tensor_tensor(same[:, 1:E], rows_f[0:BH, 1:E], rows_f[0:BH, 0:E - 1], ALU.is_equal))
                dve.tensor_scalar(seg[:, 1:E], same[:, 1:E], -1.0, -LOWEST, ALU.add, ALU.mult)
                for t in range(NT):
                    ins = dve.tensor_scalar(pick[:, t, E:2 * E], rows_f[:, E:2 * E], iota_c[:, t:t + 1], None, ALU.is_equal)
                link(ins)
                for t in range(NT):
                    dve.scalar_tensor_tensor(out=pick[:, t, 0:E], in0=rows_f[:, 0:E], scalar=iota_c[:, t:t + 1],
                                             in1=pick[:, t, E:2 * E].bitcast(F32), op0=ALU.is_equal, op1=ALU.add)
                for t in range(ET):
                    dve.tensor_scalar(onesrc[:, t, :], iota_row, sorted_c[:, t, 0:1], None, ALU.is_equal)
                for h in range(H):
                    rows = slice(h * DH, (h + 1) * DH)
                    ins = dve.tensor_scalar(apad[rows, h::BH + H], ones[rows, 0:CB], a_c[rows, :], None, ALU.mult)
                link(ins)
                dve.sem_inc(tv_free, 1)

            def make_r():
                dve.wait_ge(m_ready, 1)
                for k in range(STEPS):
                    i = STEPS - k - 1
                    ins = dve.tensor_scalar(r_k(k), att[1 - i // 4][:, (i % 4) * D:(i % 4 + 1) * D], float(comb(STEPS, k)), None, ALU.mult)
                link(ins)
                dve.sem_inc(m_copied, 1)
                for i in range(STEPS):
                    for k in range(STEPS - i):
                        coef = DT * comb(i + k, k) + (1.0 if i == 0 and k == 0 else 0.0)
                        ins = dve.scalar_tensor_tensor(out=r_k(k), in0=qp[:, i, :], scalar=coef, in1=r_k(k), op0=ALU.mult, op1=ALU.add)
                    link(ins)
                dve.sem_inc(r_done, 1)

            def stage(col, n, ps):
                link(dve.tensor_copy(us_h[:, :, col:col + n], ps))
                link(dve.tensor_tensor(us_l[:, :, col:col + n], ps, us_h[:, :, col:col + n].bitcast(F32), ALU.subtract))
                dve.sem_inc(u_staged, 1)

            def u_copy(s, n):
                dve.wait_ge(u_ready, s + 1)
                link(dve.tensor_copy(urow(s)[0:n, :], att[1][0:n, :]))
                dve.sem_inc(u_rows, 1)

            def xt_lo(c, b):
                dve.wait_ge(xt_hi, CB * c + b + 1)
                dve.tensor_tensor(ktl[:, b % 2, 0, :], xt_bank(b)[:, :], kth[:, b % 2, 0, :].bitcast(F32), ALU.subtract).then_inc(xt_free, 1)

            def baby_lo(c, b, j):
                dve.wait_ge(left_hi, 2 * CB * c + 2 * b + j)
                dve.tensor_tensor(ktl[:, b % 2, j, :], left[(j - 1) % 2][:, :], kth[:, b % 2, j, :].bitcast(F32),
                                  ALU.subtract).then_inc(left_free, 1)

            def y_split(c, b, p, with_bias):
                dve.wait_ge(y_copied, R_JOBS * c + PAIRS * b + p + 1)
                ps = yps[:, 2 * p:2 * p + 2, :]
                rows, cols = slice(2 * p, 2 * p + 2), slice(b * D, (b + 1) * D)
                dve.tensor_tensor(y2l[:, rows, cols], ps[:, :, 2 * D:3 * D], y2h[:, rows, cols].bitcast(F32), ALU.subtract)
                if with_bias:
                    dve.tensor_tensor(y0[:, rows, cols], ps[:, :, 0:D], bias[:, rows, :], ALU.add).then_inc(y_free, 1)
                else:
                    dve.tensor_copy(y0[:, rows, cols], ps[:, :, 0:D]).then_inc(y_free, 1)

            def s_add(c, t):
                job = S_JOB + t
                dve.wait_ge(left_ready, LEFT_JOBS * c + job + 1)
                dve.tensor_tensor(y1[:, t, :], left[job % 2][:, :], y1[:, t, :], ALU.add).then_inc(left_free, 1)

            def s_split(c, t):
                dve.wait_ge(s_hi, NT * c + t + 1)
                dve.tensor_tensor(sl[:, t, :], y1[:, t, :], sh[:, t, :].bitcast(F32), ALU.subtract).then_inc(s_lo, 1)

            def gather_lo(cc, b, bank, hi, lo):
                dve.wait_ge(g_hi, CB * cc + b + 1)
                dve.tensor_tensor(lo, bank, hi.bitcast(F32), ALU.subtract).then_inc(g_lo, 1)

            def leaky(cc, p, bank):
                dve.wait_ge(q_scaled, 2 * cc + p + 1)
                dve.tensor_tensor(tt[:, 2 * p:2 * p + 2, :], bank[:, :].rearrange("p (b e) -> p b e", b=2),
                                  tt[:, 2 * p:2 * p + 2, :], ALU.max).then_inc(q_leaky, 1)

            def attend_values(cc, p, bank):
                dve.wait_ge(head_ready, 2 * cc + p + 1)
                v = vv[:, 2 * p:2 * p + 2, :].rearrange("p b e -> p (b e)")
                dve.tensor_tensor(v, bank, v, ALU.mult).then_inc(av_ready, 1)

            def u_lo(cc, t):
                dve.wait_ge(u2_hi, ET * cc + t + 1)
                dve.tensor_tensor(ul[:, t, :], att[t][:, :], uh[:, t, :].bitcast(F32), ALU.subtract).then_inc(u2_lo, 1)

            def out_add(cc, t):
                job = OUT_JOB + t
                dve.wait_ge(left_ready, LEFT_JOBS * cc + job + 1)
                dve.tensor_tensor(x1[:, t, :], left[job % 2][:, :], y0[:, t, :], ALU.add).then_inc(left_free, 1)
                dve.wait_ge(left_free, LEFT_JOBS * cc + job + 1)

            def z_add(cc, t, bank):
                dve.wait_ge(z_ready, NT * cc + t + 1)
                dve.tensor_tensor(r2[:, t, :], bank, x1[:, t, :], ALU.add).then_inc(z_sum, 1)
                dve.wait_ge(z_sum, NT * (cc + 1) + t + 1)

            def stats(k, cc, t, rows):
                for b in range(CB):
                    ins = dve.bn_stats(st[:, k, t, b, :], rows[:, b * D:(b + 1) * D])
                ins.then_inc(ln_stats[k], 1)

            def moments(k, cc, t, n):
                ts = slice(t, t + n)
                dve.wait_ge(ln_stats[k], NT * cc + t + n)
                dve.tensor_tensor(mean[:, k, ts, :], st[:, k, ts, :, 1], st[:, k, ts, :, 4], ALU.add)
                dve.tensor_tensor(both[:, k, ts, :], st[:, k, ts, :, 2], st[:, k, ts, :, 5], ALU.add)
                dve.tensor_tensor(apart[:, k, ts, :], st[:, k, ts, :, 1], st[:, k, ts, :, 4], ALU.subtract).then_inc(ln_halves[k], n)
                dve.wait_ge(ln_halves[k], NT * cc + t + n)
                dve.scalar_tensor_tensor(out=apart[:, k, ts, :], in0=apart[:, k, ts, :], scalar=0.25, in1=apart[:, k, ts, :],
                                         op0=ALU.mult, op1=ALU.mult)
                dve.tensor_scalar(ve[:, k, ts, :], both[:, k, ts, :], 1.0 / D, LN_EPS, ALU.mult, ALU.add)
                dve.tensor_scalar(mean[:, k, ts, :], mean[:, k, ts, :], -0.5, None, ALU.mult).then_inc(ln_mean[k], n)
                dve.wait_ge(ln_mean[k], NT * cc + t + n)
                dve.tensor_tensor(ve[:, k, ts, :], ve[:, k, ts, :], apart[:, k, ts, :], ALU.add).then_inc(ln_var[k], n)

            def normalise(k, cc, t, tiles):
                dve.wait_ge(ln_rstd[k], NT * cc + t + 1)
                for b in range(CB):
                    r = tiles[:, t, b * D:(b + 1) * D]
                    ins = dve.tensor_scalar(r, r, mean[:, k, t, b:b + 1], rstd[:, k, t, b:b + 1], ALU.add, ALU.mult)
                ins.then_inc(ln_dve[k], 1)

            def x1_split(cc, t, hi, lo, done):
                dve.wait_ge(x1_hi, NT * cc + t + 1)
                dve.tensor_tensor(lo[:, t, :], x1[:, t, :], hi[:, t, :].bitcast(F32), ALU.subtract).then_inc(done, 1)

            def sm(cc, n, ins):
                ins.then_inc(sm_step, 1)
                dve.wait_ge(sm_step, SM * cc + n)

            def softmax_max(cc, bank):
                dve.wait_ge(score_ready, cc + 1)
                sm(cc, 1, dve.tensor_tensor(sme[:, :], bank, logrow[:, :], ALU.add))
                sm(cc, 2, dve.tensor_tensor_scan(smf[:, :], seg[:, 0:E], sme[:, :], LOWEST, ALU.add, ALU.max))
                sm(cc, 3, dve.tensor_tensor_scan(smg[:, ::-1], seg[:, E:0:-1], smf[:, ::-1], LOWEST, ALU.add, ALU.max))
                dve.tensor_tensor(smg[:, :], sme[:, :], smg[:, :], ALU.subtract).then_inc(sm_step, 1)

            def softmax_sum(cc):
                dve.wait_ge(sm_exp, cc + 1)
                sm(cc, 5, dve.tensor_tensor_scan(smg[:, :], same[:, :], smf[:, :], 0.0, ALU.mult, ALU.add))
                sm(cc, 6, dve.tensor_tensor_scan(sme[:, ::-1], seg[:, E:0:-1], smg[:, ::-1], LOWEST, ALU.add, ALU.max))
                sm(cc, 7, dve.reciprocal(smg[:, :], sme[:, :]))
                dve.tensor_tensor(sme[:, :], smf[:, :], smg[:, :], ALU.mult).then_inc(sm_step, 1)

            def body(c, attend):
                head = not attend
                if attend:
                    out_add(c - 1, 0)
                    stats(0, c - 1, 0, x1[:, 0, :])
                    out_add(c - 1, 1)
                    stats(0, c - 1, 1, x1[:, 1, :])
                    moments(0, c - 1, 0, 2)
                    out_add(c - 1, 2)
                    stats(0, c - 1, 2, x1[:, 2, :])
                    out_add(c - 1, 3)
                    stats(0, c - 1, 3, x1[:, 3, :])
                    moments(0, c - 1, 2, 2)
                if head:
                    power_lo(0, p1h, p1l)
                    for t in (0, 2):
                        dve.wait_ge(pn_hi, t + 1)
                        dve.tensor_tensor(pnl[:, t, :], pn[:, t, :], pnh[:, t, :].bitcast(F32), ALU.subtract).then_inc(pn_lo, 1)
                    baby_lo(c, 0, 1)
                    for t in range(NT):
                        ins = dve.tensor_reduce(u01[:, t, 1:2], pn[:, t, :], mybir.AxisListType.X, ALU.add)
                    link(ins)
                    dve.tensor_copy(us_h[:, :, 0:1], u01[:, :, 1:2])
                    rank_edges()
                    dve.tensor_tensor(us_l[:, :, 0:1], u01[:, :, 1:2], us_h[:, :, 0:1].bitcast(F32), ALU.subtract).then_inc(u_staged, 1)
                    power_lo(1, p2h, p2l)
                    baby_lo(c, 0, 2)
                    make_r()
                    power_lo(2, p3h, p3l)
                    dve.wait_ge(r_hi, 1)
                    dve.tensor_tensor(rl[:, :, :].rearrange("p j e -> p (j e)"), rf[:, :, :, :].rearrange("p j i e -> p (j i e)"),
                                      rh[:, :, :].rearrange("p j e -> p (j e)").bitcast(F32), ALU.subtract).then_inc(r_lo, 1)
                if head:
                    xt_lo(c, 0)
                    xt_lo(c, 1)
                else:
                    x1_split(c - 1, 0, x1h, x1l, x1_lo)
                    xt_lo(c, 0)
                    baby_lo(c, 0, 1)
                    x1_split(c - 1, 1, x1h, x1l, x1_lo)
                    normalise(0, c - 1, 3, x1)
                    baby_lo(c, 0, 2)
                    xt_lo(c, 1)
                    x1_split(c - 1, 2, x1h, x1l, x1_lo)
                    x1_split(c - 1, 3, x1h, x1l, x1_lo)
                baby_lo(c, 1, 1)
                baby_lo(c, 1, 2)
                if head:
                    edge_index()
                if attend:
                    gather_lo(c - 1, 0, att[0][:, :], gh[:, 0, :], gl[:, 0, :])
                    gather_lo(c - 1, 1, att[1][:, :], gh[:, 1, :], gl[:, 1, :])
                y_split(c, 0, 0, attend)
                y_split(c, 0, 1, attend)
                if head:
                    dve.wait_ge(u01_turned, 1)
                    link(dve.tensor_copy(urow(3)[0:2, :], att[1][0:2, :]))
                    dve.sem_inc(u01_rows, 1)
                    edge_onehots()
                if attend:
                    leaky(c - 1, 0, att[0])
                baby_lo(c, 2, 1)
                xt_lo(c, 2)
                if attend:
                    gather_lo(c - 1, 2, att[0][:, :], gh[:, 0, :], gl[:, 0, :])
                    gather_lo(c - 1, 3, att[1][:, :], gh[:, 1, :], gl[:, 1, :])
                baby_lo(c, 2, 2)
                if head:
                    dve.wait_ge(c_turned, 1)
                    dve.tensor_copy(crow[:, 0:BABY, :].rearrange("k s e -> k (s e)"), att[0][0:BABY, 0:BABY * D])
                    dve.tensor_copy(crow[0:1, 3, :], att[0][0:1, 3 * D:4 * D])
                    u_copy(0, 1)
                else:
                    leaky(c - 1, 1, att[0])
                y_split(c, 1, 0, attend)
                if attend:
                    softmax_max(c - 1, att[0][0:BH, 0:E])
                    softmax_sum(c - 1)
                y_split(c, 1, 1, attend)
                if head:
                    dve.wait_ge(u_turned, 1)
                    ps = att[0][:, 0:NT].rearrange("p (t n) -> p t n", n=1)
                    link(dve.tensor_copy(us_h[:, :, 2:3], ps))
                    dve.tensor_tensor(us_l[:, :, 2:3], ps, us_h[:, :, 2:3].bitcast(F32), ALU.subtract)
                    dve.tensor_copy(us_h[:, :, 1:2], us_h[:, :, 0:1].bitcast(F32))
                    link(dve.tensor_copy(us_l[:, :, 1:2], us_l[:, :, 0:1].bitcast(F32)))
                    dve.tensor_copy(us_h[:, :, 0:1], u01[:, :, 0:1])
                    link(dve.tensor_scalar(us_l[:, :, 0:1], u01[:, :, 0:1], 0.0, None, ALU.mult))
                    dve.sem_inc(u_staged, 1)
                xt_lo(c, 3)
                baby_lo(c, 3, 1)
                baby_lo(c, 3, 2)
                if head:
                    u_copy(1, BABY)
                if attend:
                    for p in range(2):
                        attend_values(c - 1, p, att[p][:, :])
                y_split(c, 2, 0, attend)
                y_split(c, 2, 1, attend)
                if head:
                    dve.wait_ge(u_turned, 2)
                    stage(0, BABY, att[0][:, 0:BABY * NT].rearrange("p (t n) -> p t n", n=BABY))
                    dve.wait_ge(logs, 1)
                    for t in range(ET):
                        ins = dve.tensor_scalar(log_rep[:, t, :], ones[:, 0:BH], log_c[:, t:t + 1], None, ALU.mult)
                    ins.then_inc(log_rep_ready, 1)
                if attend:
                    for t in range(ET):
                        u_lo(c - 1, t)
                y_split(c, 3, 0, attend)
                y_split(c, 3, 1, attend)
                if head:
                    u_copy(2, BABY)
                if attend:
                    z_add(c - 1, 0, att[0][:, :])
                    z_add(c - 1, 1, att[1][:, :])
                    stats(1, c - 1, 0, r2[:, 0, :])
                s_add(c, 0)
                if attend:
                    stats(1, c - 1, 1, r2[:, 1, :])
                s_split(c, 0)
                s_add(c, 1)
                if attend:
                    moments(1, c - 1, 0, 2)
                s_split(c, 1)
                if head:
                    dve.wait_ge(log_row_ready, 1)
                    dve.tensor_copy(logrow[:, :], att[0][0:BH, 0:E])
                s_add(c, 2)
                if attend:
                    z_add(c - 1, 2, att[0][:, :])
                s_split(c, 2)
                if attend:
                    stats(1, c - 1, 2, r2[:, 2, :])
                s_add(c, 3)
                s_split(c, 3)
                if attend:
                    z_add(c - 1, 3, att[1][:, :])
                    stats(1, c - 1, 3, r2[:, 3, :])
                    moments(1, c - 1, 2, 2)
                if head:
                    dve.wait_ge(bias_ready, 1)
                    link(dve.tensor_copy(bias[:, :, :].rearrange("p t e -> p (t e)"), att[1][:, :]))
                    dve.sem_inc(z_sum, NT)
                    for t in range(NT):
                        row = y0[:, t, :].rearrange("p (b e) -> p b e", b=CB)
                        ins = dve.tensor_tensor(row, row, bias[:, t:t + 1, :].broadcast_to([P, CB, D]), ALU.add)
                    link(ins)

            def tail(cc):
                for t in range(NT):
                    out_add(cc, t)
                    stats(0, cc, t, x1[:, t, :])
                    moments(0, cc, t, 1)
                for t in range(NT - LAST_DVE_TILES, NT):
                    normalise(0, cc, t, x1)
                for t in range(NT - LAST_DVE_TILES, NT):
                    x1_split(cc, t, y2h, y2l, x1_last)
                for b in range(CB):
                    gather_lo(cc, b, yps[:, b, :], *((gh[:, b, :], gl[:, b, :]) if b < 2 else (kth[:, 0, b - 2, :], ktl[:, 0, b - 2, :])))
                leaky(cc, 0, att[0])
                leaky(cc, 1, left[0])
                softmax_max(cc, yps[0:BH, 0, 0:E])
                softmax_sum(cc)
                for p in range(2):
                    attend_values(cc, p, yps[:, 1 + p, :])
                for p in range(2):
                    dve.wait_ge(av_hi, 2 * cc + p + 1)
                    dve.tensor_tensor(avl[:, 2 * p:2 * p + 2, :], vv[:, 2 * p:2 * p + 2, :],
                                      avh[:, 2 * p:2 * p + 2, :].bitcast(F32), ALU.subtract).then_inc(av_lo, 1)
                for t in range(ET):
                    u_lo(cc, t)
                for t in range(NT):
                    z_add(cc, t, yps[:, t, :])
                    stats(1, cc, t, r2[:, t, :])
                    moments(1, cc, t, 1)
                for t in range(NT - LAST_DVE_TILES, NT):
                    normalise(1, cc, t, r2)

            chunks(dve, body, tail)


_INS = ['x', 'adj', 'L0_gnn_alpha_train', 'L0_gnn_w', 'L0_gnn_d', 'L0_gnn_fc_in_w', 'L0_gnn_fc_in_b', 'L1_gnn_W_lin',
        'L1_gnn_W_val', 'L1_gnn_a', 'L1_gnn_W_out', 'L1_gnn_src', 'L1_gnn_dst']
_OUTS = [((16, 512, 128), 'float32')]


def kernel(**inputs):
    import numpy as _np
    import concourse.bacc as _bacc
    from concourse import mybir as _mybir
    from concourse.bass_utils import run_bass_kernel_spmd as _run

    nc = _bacc.Bacc("TRN2", target_bir_lowering=False, num_devices=1)
    arrays, args = {}, []
    for name in _INS:
        a = _np.ascontiguousarray(inputs[name])
        arrays[f"in_{name}_dram"] = a
        args.append(nc.dram_tensor(f"in_{name}_dram", a.shape, _mybir.dt.from_np(a.dtype), kind="ExternalInput").ap())
    for i, (shape, dtype) in enumerate(_OUTS):
        dt = _mybir.dt.from_np(_np.dtype(dtype))
        args.append(nc.dram_tensor(f"out_{i}_dram", shape, dt, kind="ExternalOutput").ap())
    graph_kernel(nc, *args)
    r = _run(nc, [arrays], core_ids=[0])
    got = tuple(r.results[0][f"out_{i}_dram"] for i in range(len(_OUTS)))
    return got[0]
```

```python
from contextlib import ExitStack
from math import comb

import concourse.bass as bass
from concourse import mybir

F32 = mybir.dt.float32
F32R = mybir.dt.float32r
I32 = mybir.dt.int32
U32 = mybir.dt.uint32
ALU = mybir.AluOpType
ACT = mybir.ActivationFunctionType

P = 128
STEPS = 8
DT = 1.0 / STEPS
LN_EPS = 1e-5
LOG_EPS = 1e-8
LRELU = 0.2
LOWEST = -3.0e38
BABY = 3


def graph_kernel(nc, x, adj, alpha, w, d, fc_w, fc_b, W_lin, W_val, a, W_out, src, dst, out):
    B, N, D = x.shape
    H, DH = a.shape
    E = src.shape[0]
    NT = N // P
    ET = E // P
    CB = 512 // D
    CHUNKS = B // CB
    W = CB * D
    BH = CB * H
    K = STEPS + 1
    assert D == P and H * DH == D and N == 512 and W == 512 and 2 * E == 512 and K == BABY * BABY
    S_JOB, OUT_JOB, LEFT_JOBS = 2 * CB, 2 * CB + NT, 2 * CB + 2 * NT
    PAIRS = NT // 2
    R_JOBS = CB * PAIRS
    SM = 8

    x_v = x.rearrange("(c b) (t p) d -> c t p b d", b=CB, p=P)
    out_v = out.rearrange("(c b) (t p) d -> c t p b d", b=CB, p=P)
    adj_v = adj.rearrange("(t p) m -> t p m", p=P)

    ctx = ExitStack()
    with ctx:
        def sb(name, shape, dt=F32):
            return ctx.enter_context(nc.sbuf_tensor(name, shape, dt))

        def sem(name):
            return ctx.enter_context(nc.semaphore(name))

        p1h, p1l = sb("p1h", [P, NT, N], F32R), sb("p1l", [P, NT, N], F32R)
        p2h, p2l = sb("p2h", [P, NT, N], F32R), sb("p2l", [P, NT, N], F32R)
        p3h, p3l = sb("p3h", [P, NT, N], F32R), sb("p3l", [P, NT, N], F32R)
        xraw = sb("xraw", [P, NT, W])
        xh, xl = sb("xh", [P, 2, NT, D], F32R), sb("xl", [P, 2, NT, D], F32R)
        kth, ktl = sb("kth", [P, 2, BABY, N], F32R), sb("ktl", [P, 2, BABY, N], F32R)
        y0, y1 = sb("y0", [P, NT, W]), sb("y1", [P, NT, W])
        y2h, y2l = sb("y2h", [P, NT, W], F32R), sb("y2l", [P, NT, W], F32R)
        sh, sl = sb("sh", [P, NT, W], F32R), sb("sl", [P, NT, W], F32R)
        x1 = sb("x1", [P, NT, W])
        rh, rl = sb("rh", [P, BABY, BABY * D], F32R), sb("rl", [P, BABY, BABY * D], F32R)
        bias = sb("bias", [P, NT, D])
        pick = sb("pick", [P, NT, 2 * E], F32R)
        onesrc = sb("onesrc", [P, ET, N], F32R)
        gh, gl = sb("gh", [P, 2, 2 * E], F32R), sb("gl", [P, 2, 2 * E], F32R)
        tv = sb("tv", [P, 2 * W * 2])
        avh, avl = sb("avh", [P, CB, E], F32R), sb("avl", [P, CB, E], F32R)
        wh, wl = sb("wh", [P, 3, D], F32R), sb("wl", [P, 3, D], F32R)
        apad = sb("apad", [P, CB * BH])
        headrow = sb("headrow", [BH, CB, D], F32R)
        attn_h, attn_l = sb("attn_h", [BH, E], F32R), sb("attn_l", [BH, E], F32R)
        logrow = sb("logrow", [BH, E])
        seg = sb("seg", [BH, E + 1])
        same = sb("same", [BH, E])
        sme, smf, smg = sb("sme", [BH, E]), sb("smf", [BH, E]), sb("smg", [BH, E])
        ident, ident_r = sb("ident", [P, P]), sb("ident_r", [P, P], F32R)
        st = sb("st", [P, 2, NT, CB, 6])
        moment = sb("moment", [P, 2, NT, CB, 2])
        nhalf, eps = sb("nhalf", [P, 2, CB]), sb("eps", [P, 2, CB])
        rstd = sb("rstd", [P, 2, NT, CB])
        shift = sb("shift", [P, 2, NT, CB])
        small = sb("small", [P, 96])

        tt = tv[:, 0:CB * E].rearrange("p (b e) -> p b e", b=CB)
        vv = tv[:, CB * E:2 * CB * E].rearrange("p (b e) -> p b e", b=CB)
        r2 = tv[:, 0:NT * W].rearrange("p (t w) -> p t w", t=NT)
        uh, ul = gh, gl
        x1h, x1l = sh, sl

        pn = x1
        pnh, pnl = y2h, y2l
        y0f = y0[:, :, :].rearrange("p t w -> p (t w)")
        y1f = y1[:, :, :].rearrange("p t w -> p (t w)")
        qp = y0f[:, 0:K * D].rearrange("p (i e) -> p i e", i=K)
        nat = y0f[:, K * D:K * D + 5 * D].rearrange("p (i e) -> p i e", i=5)
        rf = y1f[:, 0:K * D].rearrange("p (j i e) -> p j i e", j=BABY, i=BABY)
        wt = y1f[:, K * D:K * D + D]
        wtd = y1f[:, K * D + D:K * D + 2 * D]
        edge_ops = tv
        iota_row = edge_ops[:, 0:N]
        rows_i = edge_ops[:, N:N + 2 * E].bitcast(I32)
        perm = edge_ops[:, N:N + ET * E].rearrange("p (t r) -> p t r", t=ET)
        rows_f = edge_ops[:, 2 * N:2 * N + 2 * E]
        rep = edge_ops[:, 3 * N:3 * N + 2 * ET * P].rearrange("p (s t q) -> p s t q", s=2, t=ET)
        heads = rep[0:BH, :, :, :].rearrange("q s t e -> q (s t) e")
        alpha_c, exp_c, half_c, diag_c = (small[:, 4 * i:4 * i + 4] for i in range(4))
        d_c, b_c, a_c = small[:, 16:17], small[:, 17:18], small[:, 18:19]
        iota_c = small[:, 20:24]
        cols_i = small[:, 24:28].bitcast(I32)
        cols_f = small[:, 28:32]
        key_c = small[:, 32:34]
        rank_c = small[:, 34:36]
        sorted_c = small[:, 36:40].rearrange("p (t s) -> p t s", t=ET)
        idx_f = small[:, 40:42]
        idx_u = small[:, 42:44].bitcast(U32)
        a_edge = small[:, 44:46]
        log_c = small[:, 46:48]
        log_rep = small[:, 60:92].rearrange("p (t q) -> p t q", t=ET)
        ones = sb("ones", [P, P])
        log_eps = small[:, 92:93]
        u012 = sb("u012", [P, NT, 2 * BABY])
        staged = avh
        urows, c_cols, c_rows = x1[:, 0, :], bias[:, 0, :], bias[:, 1, :]
        pick_rows = sb("pick_rows", [P, BABY, BABY])

        def ROW(s):
            return 32 * s

        def r_k(k):
            return rf[:, k % BABY, k // BABY, :]

        left = [ctx.enter_context(nc.psum_tensor(f"left{i}", [P, 512], F32)) for i in range(2)]
        yps = ctx.enter_context(nc.psum_tensor("yps", [P, 4, 512], F32))
        att = [ctx.enter_context(nc.psum_tensor(f"att{i}", [P, 512], F32)) for i in range(2)]

        adj_loaded = [sem(f"adj_loaded{t}") for t in range(NT)]
        alpha_loaded, gnn_loaded = sem("alpha_loaded"), sem("gnn_loaded")
        att_loaded, edges_loaded = sem("att_loaded"), sem("edges_loaded")
        ident_ready, consts = sem("ident_ready"), sem("consts")
        const_step = sem("const_step")
        dve_step = sem("dve_step")
        exp_alpha = sem("exp_alpha")
        keys_ranked = sem("keys_ranked")
        rows_sorted, rows_copied = sem("rows_sorted"), sem("rows_copied")
        idx_ready, adj_picked, logs = sem("idx_ready"), sem("adj_picked"), sem("logs")
        log_rep_ready, log_row_ready = sem("log_rep_ready"), sem("log_row_ready")
        w_turned, w_hi, wt_ready = sem("w_turned"), sem("w_hi"), sem("wt_ready")
        q_product, q_copied = sem("q_product"), sem("q_copied")
        m_ready, m_copied, r_done, r_hi, r_lo = sem("m_ready"), sem("m_copied"), sem("r_done"), sem("r_hi"), sem("r_lo")
        ones_ready = sem("ones_ready")
        half_ready, pn_scaled = sem("half_ready"), sem("pn_scaled")
        pn_ready, pn_hi, pn_lo = sem("pn_ready"), sem("pn_hi"), sem("pn_lo")
        pow_ready, pow_hi, pow_lo = sem("pow_ready"), sem("pow_hi"), sem("pow_lo")
        u_staged, u_ready, u_rows, u_turned = sem("u_staged"), sem("u_ready"), sem("u_rows"), sem("u_turned")
        u012_turned, c_turned = sem("u012_turned"), sem("c_turned")
        bias_ready = sem("bias_ready")
        x_loaded = sem("x_loaded")
        x_hi, x_lo = sem("x_hi"), sem("x_lo")
        x_free = sem("x_free")
        x_slot = sem("x_slot")
        left_ready, left_free = sem("left_ready"), sem("left_free")
        left_hi = sem("left_hi")
        xt_ready, xt_hi, xt_free = sem("xt_ready"), sem("xt_hi"), sem("xt_free")
        y_ready, y_copied, y_free = sem("y_ready"), sem("y_copied"), sem("y_free")
        s_hi, s_lo = sem("s_hi"), sem("s_lo")
        ln_stats = [sem("ln1_stats"), sem("ln2_stats")]
        ln_turn = [sem("ln1_turn"), sem("ln2_turn")]
        ln_var = [sem("ln1_var"), sem("ln2_var")]
        ln_fixed = [sem("ln1_fixed"), sem("ln2_fixed")]
        ln_rstd = [sem("ln1_rstd"), sem("ln2_rstd")]
        ln_shift = [sem("ln1_shift"), sem("ln2_shift")]
        ln_done = [sem("ln1_done"), sem("ln2_done")]
        ln_dve = [sem("ln1_dve"), sem("ln2_dve")]
        x1_hi, x1_lo = sem("x1_hi"), sem("x1_lo")
        x1_last = sem("x1_last")
        g_ready, g_hi, g_lo = sem("g_ready"), sem("g_hi"), sem("g_lo")
        lin_ready = sem("lin_ready")
        q_scaled, q_leaky, v_copied = sem("q_scaled"), sem("q_leaky"), sem("v_copied")
        score_ready, sm_step, sm_exp = sem("score_ready"), sem("sm_step"), sem("sm_exp")
        attn_ready = sem("attn_ready")
        head_ready, av_ready, av_hi, av_lo = sem("head_ready"), sem("av_ready"), sem("av_hi"), sem("av_lo")
        u2_ready, u2_hi, u2_lo = sem("u2_ready"), sem("u2_hi"), sem("u2_lo")
        z_ready, z_sum = sem("z_ready"), sem("z_sum")
        stored = sem("stored")
        tv_free = sem("tv_free")

        def need(eng, s, value):
            if not isinstance(value, int) or value > 0:
                eng.wait_ge(s, value)

        def xt_bank(b):
            return att[(0, 1, 1, 1)[b]]

        def last_bank(t):
            return (left[0], left[1], yps[:, 3, :], yps[:, 0, :])[t]

        def passes(h1, l1, h2, l2):
            return ((h1, h2), (h1, l2), (l1, h2))

        def chunks(eng, body, tail):
            body(0, False)
            with eng.Fori(1, CHUNKS) as c:
                body(c, True)
            tail(CHUNKS - 1)

        block = ctx.enter_context(nc.Block())

        @block.sync
        def _(sp):
            def load_x(c):
                for t in range(NT):
                    sp.dma_start(xraw[:, t, :].rearrange("p (b d) -> p b d", b=CB), x_v[c, t]).then_inc(x_loaded, 16)

            def reload_x(c):
                sp.wait_ge(xt_ready, CB * c)
                sp.sem_inc(x_free, 1)
                sp.wait_ge(x_lo, CB * c)
                sp.sem_inc(x_free, 1)
                load_x(c)

            def store(cc, last=False):
                for t in range(NT):
                    if last and t >= PAIRS:
                        sp.wait_ge(ln_dve[1], t - PAIRS + 1)
                    else:
                        sp.wait_ge(ln_done[1], NT * cc + t + 1)
                    sp.dma_start(out_v[cc, t], r2[:, t, :].rearrange("p (b d) -> p b d", b=CB)).then_inc(stored, 16)
                sp.wait_ge(stored, 16 * NT * (cc + 1))
                sp.sem_inc(tv_free, 1)

            for t in range(NT):
                sp.dma_start(pn[:, t, :], adj_v[t]).then_inc(adj_loaded[t], 16)
            load_x(0)
            for s, e in enumerate((src, dst)):
                sp.dma_start(rows_i[:, s * E:(s + 1) * E], e.rearrange("(o e) -> o e", o=1).broadcast_to([P, E])).then_inc(edges_loaded, 16)
                sp.dma_start(cols_i[:, 2 * s:2 * s + 2], e.rearrange("(t p) -> p t", p=P),
                             allow_slow_non_contiguous=True).then_inc(edges_loaded, 16)
            for i, m in enumerate((W_lin, W_val, W_out)):
                sp.dma_start(nat[:, 2 + i, :], m).then_inc(att_loaded, 16)
            sp.dma_start(a_c, a.rearrange("h (e o) -> (h e) o", o=1)).then_inc(att_loaded, 16)

            reload_x(1)
            with sp.Fori(1, CHUNKS - 1) as c:
                reload_x(c + 1)
                store(c - 1)
            store(CHUNKS - 2)
            store(CHUNKS - 1, True)

        @block.gpsimd
        def _(pool):
            pool.memset(ident[:, :], 0.0).then_inc(const_step, 1)
            pool.wait_ge(const_step, 1)
            pool.affine_select(out=ident[:, :], in_=ident[:, :], compare_op=ALU.not_equal, fill=1.0,
                               base=0, pattern=[[-1, P]], channel_multiplier=1).then_inc(ident_ready, 1)
            pool.memset(heads, 1.0).then_inc(const_step, 1)
            pool.iota(iota_row, pattern=[[1, N]], base=0, channel_multiplier=0,
                      allow_small_or_imprecise_dtypes=True).then_inc(consts, 1)
            pool.iota(iota_c, pattern=[[P, NT]], base=0, channel_multiplier=1,
                      allow_small_or_imprecise_dtypes=True).then_inc(consts, 1)
            pool.wait_ge(const_step, 2)
            by_head = heads.rearrange("q b (h e) -> q b h e", h=H)
            pool.affine_select(out=by_head, in_=by_head, compare_op=ALU.is_equal, fill=0.0,
                               base=0, pattern=[[-H, CB], [-1, H], [0, DH]], channel_multiplier=1).then_inc(consts, 1)
            pool.memset(eps[:, :, :], LN_EPS)
            pool.memset(nhalf[:, :, :], -0.5).then_inc(consts, 1)

            def split_x(c, b):
                if b >= 2 or not isinstance(c, int):
                    pool.wait_ge(left_ready, LEFT_JOBS * c + 2 * (b - 1) if b >= 2 else LEFT_JOBS * (c - 1) + 2 * (b + 3))
                pool.sem_inc(x_slot, 1)
                pool.tensor_copy(xh[:, b % 2, :, :], xraw[:, :, b * D:(b + 1) * D]).then_inc(x_hi, 1)
                pool.wait_ge(x_hi, CB * c + b + 1)
                pool.tensor_tensor(xl[:, b % 2, :, :], xraw[:, :, b * D:(b + 1) * D],
                                   xh[:, b % 2, :, :].bitcast(F32), ALU.subtract).then_inc(x_lo, 1)

            def rsqrt(k, cc, t, n):
                ts = slice(t, t + n)
                pool.wait_ge(ln_var[k], NT * cc + t + n)
                var = moment[:, k, ts, :, 1]
                neg_mean = moment[:, k, ts, :, 0]
                pool.tensor_tensor(var, var, eps[:, 0:n, :], ALU.add).then_inc(ln_fixed[k], n)
                pool.tensor_scalar(neg_mean, neg_mean, -1.0, None, ALU.mult).then_inc(ln_fixed[k], n)
                pool.wait_ge(ln_fixed[k], 2 * (NT * cc + t + n))
                pool.tensor_tensor(rstd[:, k, ts, :], var, nhalf[:, 0:n, :], ALU.pow).then_inc(ln_rstd[k], n)
                pool.wait_ge(ln_rstd[k], NT * cc + t + n)
                pool.tensor_tensor(shift[:, k, ts, :], neg_mean, rstd[:, k, ts, :], ALU.mult).then_inc(ln_shift[k], n)

            def body(c, attend):
                head = not attend
                pool.wait_ge(x_loaded, 16 * NT * (c + 1))
                if head:
                    pool.wait_ge(x_lo, 1)
                    for t in (1, 3):
                        pool.wait_ge(pn_hi, t + 1)
                        pool.tensor_tensor(pnl[:, t, :], pn[:, t, :], pnh[:, t, :].bitcast(F32), ALU.subtract).then_inc(pn_lo, 1)
                else:
                    split_x(c, 0)
                    rsqrt(0, c - 1, 0, 2)
                split_x(c, 1)
                if attend:
                    rsqrt(0, c - 1, 2, 2)
                split_x(c, 2)
                if head:
                    pool.wait_ge(idx_ready, 1)
                    adj_flat = adj.rearrange("n (m o) -> (n m) o", o=1)
                    for t in range(ET):
                        pool.indirect_dma_start(a_edge[:, t:t + 1], None, adj_flat,
                                                bass.IndirectOffsetOnAxis(ap=idx_u[:, t:t + 1], axis=0)).then_inc(adj_picked, 16)
                split_x(c, 3)
                if attend:
                    for p in range(2):
                        pool.wait_ge(av_hi, 2 * (c - 1) + p + 1)
                        pool.tensor_tensor(avl[:, 2 * p:2 * p + 2, :], vv[:, 2 * p:2 * p + 2, :],
                                           avh[:, 2 * p:2 * p + 2, :].bitcast(F32), ALU.subtract).then_inc(av_lo, 1)
                    rsqrt(1, c - 1, 0, 2)
                    rsqrt(1, c - 1, 2, 2)

            def x1_split(cc, t):
                pool.wait_ge(x1_hi, NT * cc + t + 1)
                pool.tensor_tensor(y2l[:, t, :], x1[:, t, :], y2h[:, t, :].bitcast(F32), ALU.subtract).then_inc(x1_lo, 1)

            def tail(cc):
                rsqrt(0, cc, 0, 1)
                rsqrt(0, cc, 1, 1)
                x1_split(cc, 0)
                rsqrt(0, cc, 2, 1)
                rsqrt(0, cc, 3, 1)
                for t in range(NT):
                    rsqrt(1, cc, t, 1)

            chunks(pool, body, tail)

        @block.scalar
        def _(act):
            col = "(p o) -> p o"
            act.dma_start(alpha_c, alpha.rearrange("(t p) -> p t", p=P), allow_slow_non_contiguous=True).then_inc(alpha_loaded, 16)
            act.wait_ge(ones_ready, 1)
            act.activation(small[:, 93:94], ones[:, 0:1], ACT.Exp)
            act.dma_start(nat[:, 0, :], w).then_inc(gnn_loaded, 16)
            act.dma_start(nat[:, 1, :], fc_w).then_inc(gnn_loaded, 16)
            act.dma_start(d_c, d.rearrange(col, o=1)).then_inc(gnn_loaded, 16)
            act.dma_start(b_c, fc_b.rearrange(col, o=1)).then_inc(gnn_loaded, 16)
            act.wait_ge(alpha_loaded, 16)
            act.activation(exp_c, alpha_c, ACT.Exp, scale=-1.0).then_inc(exp_alpha, 1)
            act.wait_ge(half_ready, 1)
            for t in range(PAIRS, NT):
                act.wait_ge(adj_loaded[t], 16)
                act.activation(pn[:, t, :], pn[:, t, :], ACT.Copy, scale=half_c[:, t:t + 1]).then_inc(pn_scaled, 1)
            for t in range(NT):
                act.wait_ge(pn_ready, t + 1)
                act.activation(pnh[:, t, :], pn[:, t, :], ACT.Copy).then_inc(pn_hi, 1)

            def power_hi(n, ph, tiles=range(NT)):
                for t in tiles:
                    act.wait_ge(pow_ready, NT * n + t + 1)
                    act.activation(ph[:, t, :], yps[:, t, :], ACT.Copy).then_inc(pow_hi, 1)

            def xt_copy(c, b):
                need(act, y_ready, R_JOBS * c + PAIRS * (b - 1))
                act.wait_ge(xt_ready, CB * c + b + 1)
                act.activation(kth[:, b % 2, 0, :], xt_bank(b)[:, :], ACT.Copy).then_inc(xt_hi, 1)

            def baby_hi(c, b, j):
                act.wait_ge(left_ready, LEFT_JOBS * c + 2 * b + j)
                act.activation(kth[:, b % 2, j, :], left[(j - 1) % 2][:, :], ACT.Copy).then_inc(left_hi, 1)

            def normalise(k, cc, t, tiles, bank=None):
                act.wait_ge(ln_shift[k], NT * cc + t + 1)
                for b in range(CB):
                    cols = slice(b * D, (b + 1) * D)
                    ins = act.activation(tiles[:, t, cols], (tiles[:, t, cols] if bank is None else bank[:, cols]), ACT.Identity,
                                         bias=shift[:, k, t, b:b + 1], scale=rstd[:, k, t, b:b + 1])
                ins.then_inc(ln_done[k], 1)

            def x1_copy(cc, t, hi=x1h, dve_tiles=(NT - 1,)):
                if t in dve_tiles:
                    act.wait_ge(ln_dve[0], cc + dve_tiles.index(t) + 1)
                else:
                    act.wait_ge(ln_done[0], (NT - 1) * cc + sum(i not in dve_tiles for i in range(t)) + 1)
                act.activation(hi[:, t, :], x1[:, t, :], ACT.Copy).then_inc(x1_hi, 1)

            def y_copy(c, b, p):
                act.wait_ge(y_ready, R_JOBS * c + PAIRS * b + p + 1)
                ps = yps[:, 2 * p:2 * p + 2, :]
                act.activation(y2h[:, 2 * p:2 * p + 2, b * D:(b + 1) * D], ps[:, :, 2 * D:3 * D], ACT.Copy)
                act.activation(y1[:, 2 * p:2 * p + 2, b * D:(b + 1) * D], ps[:, :, D:2 * D], ACT.Copy).then_inc(y_copied, 1)

            def gather_hi(cc, b, bank, slot):
                act.wait_ge(g_ready, CB * cc + b + 1)
                act.activation(slot, bank, ACT.Copy).then_inc(g_hi, 1)

            def lin(cc, p, q_bank, v_bank):
                if p == 0:
                    act.wait_ge(tv_free, cc + 1)
                act.wait_ge(lin_ready, 4 * cc + 2 * p + 1)
                act.activation(tt[:, 2 * p:2 * p + 2, :], q_bank[:, :].rearrange("p (b e) -> p b e", b=2),
                               ACT.Copy, scale=LRELU).then_inc(q_scaled, 1)
                act.wait_ge(lin_ready, 4 * cc + 2 * p + 2)
                act.activation(vv[:, 2 * p:2 * p + 2, :], v_bank[:, :].rearrange("p (b e) -> p b e", b=2),
                               ACT.Copy).then_inc(v_copied, 1)

            def exponential(cc):
                act.wait_ge(sm_step, SM * cc + 4)
                act.activation(smf[:, :], smg[:, :], ACT.Exp).then_inc(sm_exp, 1)

            def av_copy(cc, p):
                act.wait_ge(av_ready, 2 * cc + p + 1)
                act.activation(avh[:, 2 * p:2 * p + 2, :], vv[:, 2 * p:2 * p + 2, :], ACT.Copy).then_inc(av_hi, 1)

            def u_hi(cc, t):
                act.wait_ge(u2_ready, ET * cc + t + 1)
                act.activation(uh[:, t, :], att[t][:, :], ACT.Copy).then_inc(u2_hi, 1)

            def body(c, attend):
                head = not attend
                if head:
                    power_hi(0, p1h)
                    act.wait_ge(q_product, 1)
                    act.activation(qp[:, 1, :], att[0][:, 2 * D:3 * D], ACT.Copy, scale=DT).then_inc(q_copied, 1)
                    baby_hi(c, 0, 1)
                    act.wait_ge(q_product, 2)
                    act.activation(qp[:, 2, :], att[0][:, 3 * D:4 * D], ACT.Copy).then_inc(q_copied, 1)
                    power_hi(1, p2h, (0, 1))
                    act.wait_ge(q_product, 3)
                    act.activation(qp[:, 3:5, :].rearrange("p i e -> p (i e)"), att[1][:, 0:2 * D], ACT.Copy).then_inc(q_copied, 1)
                    power_hi(1, p2h, (2, 3))
                    act.wait_ge(q_product, 4)
                    act.activation(qp[:, 5:9, :].rearrange("p i e -> p (i e)"), att[0][:, :], ACT.Copy).then_inc(q_copied, 1)
                    baby_hi(c, 0, 2)
                    power_hi(2, p3h)
                    act.wait_ge(r_done, 1)
                    act.activation(rh[:, :, :], rf[:, :, :, :].rearrange("p j i e -> p j (i e)"), ACT.Copy).then_inc(r_hi, 1)
                xt_copy(c, 0)
                if head:
                    xt_copy(c, 1)
                else:
                    act.wait_ge(left_ready, LEFT_JOBS * c)
                    normalise(0, c - 1, 0, x1)
                    x1_copy(c - 1, 0)
                    baby_hi(c, 0, 1)
                    normalise(0, c - 1, 1, x1)
                    baby_hi(c, 0, 2)
                    x1_copy(c - 1, 1)
                    xt_copy(c, 1)
                    normalise(0, c - 1, 2, x1)
                    x1_copy(c - 1, 2)
                    x1_copy(c - 1, 3)
                baby_hi(c, 1, 1)
                baby_hi(c, 1, 2)
                if head:
                    act.wait_ge(w_turned, 2)
                    act.activation(wh[:, :, :].rearrange("p i e -> p (i e)"), att[0][:, 0:3 * D], ACT.Copy).then_inc(w_hi, 1)
                if attend:
                    gather_hi(c - 1, 0, att[0][:, :], gh[:, 0, :])
                    gather_hi(c - 1, 1, att[1][:, :], gh[:, 1, :])
                y_copy(c, 0, 0)
                y_copy(c, 0, 1)
                if attend:
                    lin(c - 1, 0, *att)
                baby_hi(c, 2, 1)
                xt_copy(c, 2)
                if attend:
                    gather_hi(c - 1, 2, att[0][:, :], gh[:, 0, :])
                    gather_hi(c - 1, 3, att[1][:, :], gh[:, 1, :])
                baby_hi(c, 2, 2)
                if attend:
                    lin(c - 1, 1, *att)
                y_copy(c, 1, 0)
                if attend:
                    exponential(c - 1)
                y_copy(c, 1, 1)
                xt_copy(c, 3)
                baby_hi(c, 3, 1)
                baby_hi(c, 3, 2)
                if head:
                    act.wait_ge(adj_picked, 16 * ET)
                    act.activation(log_c, a_edge, ACT.Ln, bias=log_eps).then_inc(logs, 1)
                if attend:
                    for p in range(2):
                        av_copy(c - 1, p)
                y_copy(c, 2, 0)
                y_copy(c, 2, 1)
                if attend:
                    for t in range(ET):
                        u_hi(c - 1, t)
                y_copy(c, 3, 0)
                y_copy(c, 3, 1)
                for t in range(NT):
                    act.wait_ge(left_free, LEFT_JOBS * c + S_JOB + t + 1)
                    act.activation(sh[:, t, :], y1[:, t, :], ACT.Copy).then_inc(s_hi, 1)
                if attend:
                    for t in range(NT):
                        normalise(1, c - 1, t, r2)

            def tail(cc):
                for t in range(NT):
                    if t in (1, 2):
                        normalise(0, cc, t, x1)
                    x1_copy(cc, t, y2h, (0, NT - 1))
                for b in range(CB):
                    gather_hi(cc, b, yps[:, b, :], (gh[:, b, :] if b < 2 else kth[:, 0, b - 2, :]))
                lin(cc, 0, *att)
                lin(cc, 1, *left)
                exponential(cc)
                for p in range(2):
                    av_copy(cc, p)
                for t in range(ET):
                    u_hi(cc, t)
                for t in range(PAIRS):
                    normalise(1, cc, t, r2, last_bank(t))

            chunks(act, body, tail)

        @block.tensor
        def _(pe):
            def flat(ap):
                return ap.rearrange("p i e -> p (i e)")

            def accumulate(out_ap, todo):
                for i, (l, r) in enumerate(todo):
                    mm = pe.matmul(out_ap, l, r, start=(i == 0), stop=(i == len(todo) - 1))
                return mm

            pe.wait_ge(ident_ready, 1)
            pe.wait_ge(gnn_loaded, 64)
            for i in range(2):
                mm = pe.transpose(att[0][:, i * D:(i + 1) * D], nat[:, i, :], ident[:, :])
            mm.then_inc(w_turned, 1)
            for n in range(NT):
                pe.wait_ge(pn_ready, n + 1)
                for t in range(NT):
                    mm = pe.transpose(yps[:, t, n * P:(n + 1) * P], pn[:, n, t * P:(t + 1) * P], ident[:, :])
                    if n == NT - 1:
                        mm.then_inc(pow_ready, 1)
            pe.wait_ge(wt_ready, 1)
            pe.matmul(att[0][:, 2 * D:3 * D], wtd, wt, start=True, stop=True).then_inc(q_product, 1)

            def power(n, ph, pl, tiles=range(NT)):
                pe.wait_ge(pow_lo, NT * (n - 1))
                for t in tiles:
                    cols = slice(t * P, (t + 1) * P)
                    accumulate(yps[:, t, :], [q for k in range(NT) for q in passes(
                        pnh[:, k, cols], pnl[:, k, cols], ph[:, k, :], pl[:, k, :])]).then_inc(pow_ready, 1)

            def u_step(s, ph, pl):
                pe.wait_ge(u_staged, s + 1)
                accumulate(att[1][:, :], [(staged[:, m, 0:P], x[:, m, :]) for m in range(NT) for x in (ph, pl)]).then_inc(u_ready, 1)

            def turn(s, n):
                pe.wait_ge(u_rows, s + 1)
                for t in range(NT):
                    mm = pe.matmul(att[0][:, n * t:n * t + n], urows[:, t * P:(t + 1) * P], pick_rows[:, s, 0:n], start=True, stop=True)
                mm.then_inc(u_turned, 1)

            def left_bank(c, job):
                need(pe, left_free, LEFT_JOBS * c + job - 1)
                return left[job % 2]

            def turn_x(c, b):
                for t in range(NT):
                    mm = pe.transpose(xt_bank(b)[:, t * P:(t + 1) * P], xraw[:, t, b * D:(b + 1) * D], ident[:, :])
                mm.then_inc(xt_ready, 1)

            def baby(c, b, j, ph, pl, split_from=None):
                pe.wait_ge(x_lo, CB * c + b + 1)
                ps = left_bank(c, 2 * b + j - 1)
                for m in range(NT):
                    if split_from is not None:
                        pe.wait_ge(pow_lo, split_from + m + 1)
                    for i, (l, r) in enumerate(passes(xh[:, b % 2, m, :], xl[:, b % 2, m, :], ph[:, m, :], pl[:, m, :])):
                        mm = pe.matmul(ps[:, :], l, r, start=(m == 0 and i == 0), stop=(m == NT - 1 and i == 2))
                mm.then_inc(left_ready, 1)

            def rights(c, b, p):
                if p == 0:
                    pe.wait_ge(xt_free, CB * c + b + 1)
                    pe.wait_ge(left_free, LEFT_JOBS * c + 2 * (b + 1))
                need(pe, y_free, R_JOBS * c + PAIRS * b + p - 1)
                for n in (2 * p, 2 * p + 1):
                    cols = slice(n * P, (n + 1) * P)
                    mm = accumulate(yps[:, n, 0:BABY * D], [q for j in range(BABY) for q in passes(
                        kth[:, b % 2, j, cols], ktl[:, b % 2, j, cols], rh[:, j, :], rl[:, j, :])])
                mm.then_inc(y_ready, 1)

            def giant(c, job, n, zh, zl, arrived, count):
                ps = left_bank(c, job)
                cols = slice(n * P, (n + 1) * P)
                for m in range(NT):
                    if n == 0 and count(m) is not None:
                        pe.wait_ge(arrived, count(m))
                    for i, (l, r) in enumerate(passes(p3h[:, m, cols], p3l[:, m, cols], zh[:, m, :], zl[:, m, :])):
                        mm = pe.matmul(ps[:, :], l, r, start=(m == 0 and i == 0), stop=(m == NT - 1 and i == 2))
                mm.then_inc(left_ready, 1)

            def gather(cc, b):
                cols = slice(b * D, (b + 1) * D)
                accumulate(att[b % 2][:, :], [(x[:, t, cols], pick[:, t, :]) for t in range(NT) for x in (x1h, x1l)]).then_inc(g_ready, 1)

            def lin(cc, p, hi, lo, banks):
                pe.wait_ge(g_lo, CB * cc + 2 * p + 2)
                for i in range(2):
                    cols = slice(i * E, (i + 1) * E)
                    accumulate(banks[i][:, :].rearrange("p (b e) -> p b e", b=2),
                               passes(wh[:, i, :], wl[:, i, :], hi[:, 0:2, cols], lo[:, 0:2, cols])).then_inc(lin_ready, 1)

            def scores(cc, bank):
                pe.wait_ge(q_leaky, 2 * (cc + 1))
                accumulate(bank, [(apad[:, b * BH:(b + 1) * BH], tt[:, b, :]) for b in range(CB)]).then_inc(score_ready, 1)

            def attention(cc, *banks):
                pe.wait_ge(attn_ready, cc + 1)
                pe.wait_ge(v_copied, 2 * (cc + 1))
                for p in range(2):
                    for b in (2 * p, 2 * p + 1):
                        mm = accumulate(banks[p][:, (b % 2) * E:(b % 2 + 1) * E], [(headrow[:, b, :], x) for x in (attn_h[:, :], attn_l[:, :])])
                    mm.then_inc(head_ready, 1)

            def u_tile(cc, t):
                es = slice(t * P, (t + 1) * P)
                for b in range(CB):
                    if t == 0:
                        pe.wait_ge(av_lo, 2 * cc + b // 2 + 1)
                    mm = accumulate(att[t][:, b * D:(b + 1) * D], passes(avh[:, b, es], avl[:, b, es], wh[:, 2, :], wl[:, 2, :]))
                mm.then_inc(u2_ready, 1)

            def z_sums(cc, n, bank):
                if n == 0:
                    pe.wait_ge(u2_lo, ET * (cc + 1))
                cols = slice(n * P, (n + 1) * P)
                accumulate(bank, [(onesrc[:, t, cols], u[:, t, :]) for t in range(ET) for u in (uh, ul)]).then_inc(z_ready, 1)

            def s_tile(c, t):
                giant(c, S_JOB + t, t, y2h, y2l, y_free, lambda m: R_JOBS * c + R_JOBS - 1 + m // 2 if m % 2 == 0 else None)

            def out_tile(c, t):
                giant(c, OUT_JOB + t, t, sh, sl, s_lo, lambda m: NT * c + m + 1)

            def body(c, attend):
                head = not attend
                if attend:
                    out_tile(c - 1, 0)
                    pe.wait_ge(x_loaded, 16 * NT * (c + 1))
                    pe.wait_ge(z_sum, NT * (c - 1) + 3)
                    turn_x(c, 0)
                    out_tile(c - 1, 1)
                    out_tile(c - 1, 2)
                    out_tile(c - 1, 3)
                if head:
                    baby(c, 0, 1, p1h, p1l, 0)
                    pe.wait_ge(q_copied, 1)
                    pe.matmul(att[0][:, 3 * D:4 * D], qp[:, 1, :], qp[:, 1, :], start=True, stop=True).then_inc(q_product, 1)
                    pe.wait_ge(pn_lo, NT)
                    power(2, p1h, p1l, (0, 1))
                    pe.wait_ge(q_copied, 2)
                    pe.matmul(att[1][:, 0:2 * D], qp[:, 2, :], flat(qp[:, 1:3, :]), start=True, stop=True).then_inc(q_product, 1)
                    power(2, p1h, p1l, (2, 3))
                    pe.wait_ge(q_copied, 3)
                    pe.matmul(att[0][:, :], qp[:, 4, :], flat(qp[:, 1:5, :]), start=True, stop=True).then_inc(q_product, 1)
                    baby(c, 0, 2, p2h, p2l, NT)
                    pe.wait_ge(q_copied, 4)
                    pe.matmul(att[1][:, :], nat[:, 1, :], flat(qp[:, 1:5, :]), start=True, stop=True)
                    mm = pe.matmul(att[0][:, :], nat[:, 1, :], flat(qp[:, 5:9, :]), start=True, stop=True)
                    mm.then_inc(m_ready, 1)
                    power(3, p2h, p2l)
                    pe.wait_ge(m_copied, 1)
                    turn_x(c, 0)
                    turn_x(c, 1)
                else:
                    pe.wait_ge(z_sum, NT * c)
                    turn_x(c, 1)
                    baby(c, 0, 1, p1h, p1l)
                    baby(c, 0, 2, p2h, p2l)
                baby(c, 1, 1, p1h, p1l)
                baby(c, 1, 2, p2h, p2l)
                if head:
                    pe.wait_ge(xt_free, 1)
                    pe.wait_ge(att_loaded, 64)
                    for i in range(3):
                        pe.transpose(att[0][:, i * D:(i + 1) * D], nat[:, 2 + i, :], ident[:, :])
                    pe.wait_ge(keys_ranked, 1)
                    for r in range(ET):
                        accumulate(att[0][:, 3 * D + 2 * r:3 * D + 2 * r + 2],
                                   [(perm[:, t, r * P:(r + 1) * P], cols_f[:, t::2]) for t in range(ET)])
                    for i in range(K):
                        col = 3 * D + 2 * ET + i
                        mm = pe.matmul(att[0][:, col:col + 1], qp[:, i, :], b_c, start=True, stop=True)
                    mm.then_inc(w_turned, 1)
                    pe.wait_ge(xt_free, 2)
                    for s in range(2):
                        mm = accumulate(att[1][:, s * E:(s + 1) * E], [(rep[:, s, t, :], perm[:, t, :]) for t in range(ET)])
                    mm.then_inc(rows_sorted, 1)
                    pe.wait_ge(r_lo, 1)
                    pe.wait_ge(pow_lo, 3 * NT)
                if attend:
                    pe.wait_ge(xt_free, CB * c + 2)
                    pe.wait_ge(x1_lo, NT * c)
                    gather(c - 1, 0)
                    gather(c - 1, 1)
                rights(c, 0, 0)
                rights(c, 0, 1)
                if attend:
                    lin(c - 1, 0, gh, gl, att)
                baby(c, 2, 1, p1h, p1l)
                if head:
                    pe.wait_ge(rows_copied, 1)
                else:
                    pe.wait_ge(v_copied, 2 * c - 1)
                    pe.wait_ge(q_leaky, 2 * c - 1)
                turn_x(c, 2)
                if attend:
                    gather(c - 1, 2)
                    pe.wait_ge(xt_free, CB * c + 3)
                    gather(c - 1, 3)
                baby(c, 2, 2, p2h, p2l)
                if attend:
                    lin(c - 1, 1, gh, gl, att)
                rights(c, 1, 0)
                if head:
                    pe.wait_ge(xt_free, 3)
                    u_step(0, p1h, p1l)
                    mm = pe.matmul(att[0][:, 0:P], c_cols, ident[:, :], start=True, stop=True)
                    mm.then_inc(c_turned, 1)
                if attend:
                    scores(c - 1, att[0][0:BH, 0:E])
                rights(c, 1, 1)
                if head:
                    turn(0, 1)
                else:
                    pe.wait_ge(v_copied, 2 * c)
                turn_x(c, 3)
                baby(c, 3, 1, p1h, p1l)
                baby(c, 3, 2, p2h, p2l)
                pe.wait_ge(xt_free, CB * (c + 1))
                if head:
                    u_step(1, p3h, p3l)
                    for t in range(NT):
                        mm = pe.matmul(att[0][0:2 * BABY, t * P:(t + 1) * P], u012[:, t, :], ident[:, :], start=True, stop=True)
                    mm.then_inc(u012_turned, 1)
                else:
                    attention(c - 1, *att)
                rights(c, 2, 0)
                rights(c, 2, 1)
                if head:
                    turn(1, BABY)
                else:
                    u_tile(c - 1, 0)
                    u_tile(c - 1, 1)
                rights(c, 3, 0)
                rights(c, 3, 1)
                if head:
                    u_step(2, p3h, p3l)
                else:
                    z_sums(c - 1, 0, att[0][:, :])
                    z_sums(c - 1, 1, att[1][:, :])
                s_tile(c, 0)
                s_tile(c, 1)
                if head:
                    pe.wait_ge(log_rep_ready, 1)
                    for i in range(ET):
                        mm = pe.matmul(att[0][0:BH, i * P:(i + 1) * P], log_rep[:, i, :], ident[:, :], start=True, stop=True)
                    mm.then_inc(log_row_ready, 1)
                s_tile(c, 2)
                if attend:
                    pe.wait_ge(z_sum, NT * c + 1)
                    z_sums(c - 1, 2, att[0][:, :])
                s_tile(c, 3)
                if attend:
                    pe.wait_ge(z_sum, NT * c + 2)
                    z_sums(c - 1, 3, att[1][:, :])
                if head:
                    pe.wait_ge(u_rows, 3)
                    for t in range(NT):
                        cols = slice(t * P, (t + 1) * P)
                        mm = pe.matmul(att[1][:, cols], urows[:, cols], c_rows, start=True, stop=True)
                    mm.then_inc(bias_ready, 1)

            def tail(cc):
                for t in range(NT):
                    out_tile(cc, t)
                for t in range(NT):
                    if t == 0:
                        pe.wait_ge(x1_lo, NT * cc + 1)
                    else:
                        pe.wait_ge(x1_last, t)
                    for b in range(CB):
                        cols = slice(b * D, (b + 1) * D)
                        pe.matmul(yps[:, b, :], y2h[:, t, cols], pick[:, t, :], start=(t == 0), stop=False)
                        mm = pe.matmul(yps[:, b, :], y2l[:, t, cols], pick[:, t, :], start=False, stop=(t == NT - 1))
                        if t == NT - 1:
                            mm.then_inc(g_ready, 1)
                pe.wait_ge(z_sum, NT * (cc + 1))
                lin(cc, 0, gh, gl, att)
                pe.wait_ge(left_free, LEFT_JOBS * (cc + 1))
                lin(cc, 1, kth[:, 0, :, :], ktl[:, 0, :, :], left)
                scores(cc, yps[0:BH, 0, 0:E])
                pe.wait_ge(v_copied, 2 * (cc + 1))
                for n in range(NT):
                    if n == NT - 1:
                        pe.wait_ge(sm_step, SM * cc + 1)
                    for i, x in enumerate((y2h, y2l)):
                        pe.matmul(last_bank(n)[:, :], ident_r[:, :], x[:, n, :], start=(i == 0), stop=False)
                attention(cc, yps[:, 1, :], yps[:, 2, :])
                for t in range(ET):
                    u_tile(cc, t)
                for t in range(ET):
                    pe.wait_ge(u2_lo, ET * cc + t + 1)
                    for n in range(NT):
                        cols = slice(n * P, (n + 1) * P)
                        pe.matmul(last_bank(n)[:, :], onesrc[:, t, cols], uh[:, t, :], start=False, stop=False)
                        mm = pe.matmul(last_bank(n)[:, :], onesrc[:, t, cols], ul[:, t, :], start=False, stop=(t == ET - 1))
                        if t == ET - 1:
                            mm.then_inc(z_ready, 1)

            chunks(pe, body, tail)

        @block.vector
        def _(dve):
            done = [0]

            def link(ins):
                done[0] += 1
                ins.then_inc(dve_step, 1)
                dve.wait_ge(dve_step, done[0])

            dve.memset(ones[:, :], 1.0).then_inc(ones_ready, 1)
            dve.memset(staged[:, :, :].rearrange("p t c -> p (t c)").bitcast(F32), 0.0)
            dve.memset(u012[:, :, 2:2 * BABY], 0.0)
            dve.memset(apad[:, :], 0.0)
            dve.memset(seg[:, :], LOWEST)
            dve.memset(same[:, :], 0.0)
            dve.memset(u012[:, :, 0:1], 1.0)
            dve.memset(c_cols, 0.0)
            dve.memset(log_eps, LOG_EPS).then_inc(consts, 1)
            dve.wait_ge(exp_alpha, 1)
            link(dve.tensor_scalar(exp_c, exp_c, 1.0, None, ALU.add))
            link(dve.reciprocal(half_c, exp_c))
            link(dve.tensor_scalar(half_c, half_c, DT / 2, None, ALU.mult))
            dve.sem_inc(half_ready, 1)
            link(dve.tensor_scalar(diag_c, half_c, -1.0, 1.0 - DT, ALU.mult, ALU.add))
            for t in range(PAIRS):
                dve.wait_ge(adj_loaded[t], 16)
                ins = dve.tensor_scalar(pn[:, t, :], pn[:, t, :], half_c[:, t:t + 1], None, ALU.mult)
            link(ins)
            dve.wait_ge(ident_ready, 1)
            for t in range(NT):
                if t >= PAIRS:
                    dve.wait_ge(pn_scaled, t - PAIRS + 1)
                dg = pn[:, t, t * P:(t + 1) * P]
                dve.scalar_tensor_tensor(out=dg, in0=ident[:, :], scalar=diag_c[:, t:t + 1], in1=dg,
                                         op0=ALU.mult, op1=ALU.add).then_inc(pn_ready, 1)
            dve.wait_ge(gnn_loaded, 64)
            dve.wait_ge(w_turned, 1)
            dve.tensor_scalar(d_c, d_c, 0.0, 1.0, ALU.max, ALU.min)
            link(dve.tensor_copy(wt, att[0][:, 0:D]))
            dve.tensor_scalar(wtd, wt, d_c, None, ALU.mult)
            dve.tensor_copy(r_k(STEPS), att[0][:, D:2 * D]).then_inc(wt_ready, 1)
            dve.tensor_copy(qp[:, 0, :], ident[:, :])
            for i in range(BABY):
                dve.tensor_tensor(pick_rows[:, i, :], ident[:, ROW(i):ROW(i) + BABY], ident[:, ROW(i) + BABY:ROW(i) + 2 * BABY], ALU.add)
            dve.tensor_copy(ident_r[:, :], ident[:, :])

            def power_lo(n, ph, pl):
                for t in range(NT):
                    dve.wait_ge(pow_hi, NT * n + t + 1)
                    dve.tensor_tensor(pl[:, t, :], yps[:, t, :], ph[:, t, :].bitcast(F32), ALU.subtract).then_inc(pow_lo, 1)

            def rank_edges():
                dve.wait_ge(edges_loaded, 64)
                dve.wait_ge(consts, 5)
                dve.tensor_copy(headrow[:, :, :], heads)
                dve.tensor_copy(rows_f, rows_i)
                link(dve.tensor_copy(cols_f, cols_i))
                dve.scalar_tensor_tensor(out=rows_f[:, 0:E], in0=rows_f[:, 0:E], scalar=float(E), in1=iota_row[:, 0:E], op0=ALU.mult, op1=ALU.add)
                dve.scalar_tensor_tensor(out=key_c, in0=cols_f[:, 0:2], scalar=float(E), in1=iota_c[:, 0:2], op0=ALU.mult, op1=ALU.add)
                for s in range(2):
                    for t in range(ET):
                        ins = dve.tensor_scalar(rep[:, s, t, :], ones[:, :], cols_f[:, 2 * s + t:2 * s + t + 1], None, ALU.mult)
                link(ins)
                for t in range(ET):
                    link(dve.tensor_scalar(rows_f[:, E:2 * E], rows_f[:, 0:E], key_c[:, t:t + 1], 0.0, ALU.is_lt, ALU.add,
                                           accum_out=rank_c[:, t:t + 1]))
                for t in range(ET):
                    ins = dve.tensor_scalar(perm[:, t, :], iota_row[:, 0:E], rank_c[:, t:t + 1], None, ALU.is_equal)
                ins.then_inc(keys_ranked, 1)

            def edge_index():
                dve.wait_ge(w_hi, 1)
                dve.tensor_tensor(wl[:, :, :].rearrange("p i e -> p (i e)"), att[0][:, 0:3 * D],
                                  wh[:, :, :].rearrange("p i e -> p (i e)").bitcast(F32), ALU.subtract)
                for k in range(K):
                    col = 3 * D + 2 * ET + STEPS - k
                    for i in (ROW(k // BABY) + k % BABY, ROW(k // BABY) + BABY + k % BABY)[0:1 if k < BABY else 2]:
                        dve.tensor_scalar(c_cols[:, i:i + 1], att[0][:, col:col + 1], float(comb(STEPS, k)), None, ALU.mult)
                link(dve.tensor_copy(sorted_c, att[0][:, 3 * D:3 * D + 2 * ET].rearrange("p (t s) -> p t s", t=ET)))
                link(dve.scalar_tensor_tensor(out=idx_f, in0=sorted_c[:, :, 0], scalar=float(N), in1=sorted_c[:, :, 1],
                                              op0=ALU.mult, op1=ALU.add))
                dve.tensor_copy(idx_u, idx_f).then_inc(idx_ready, 1)
                dve.wait_ge(rows_sorted, 1)
                link(dve.tensor_copy(rows_f, att[1][:, :]))
                dve.sem_inc(rows_copied, 1)

            def edge_onehots():
                link(dve.tensor_tensor(same[:, 1:E], rows_f[0:BH, 1:E], rows_f[0:BH, 0:E - 1], ALU.is_equal))
                dve.tensor_scalar(seg[:, 1:E], same[:, 1:E], -1.0, -LOWEST, ALU.add, ALU.mult)
                for t in range(NT):
                    ins = dve.tensor_scalar(pick[:, t, E:2 * E], rows_f[:, E:2 * E], iota_c[:, t:t + 1], None, ALU.is_equal)
                link(ins)
                for t in range(NT):
                    dve.scalar_tensor_tensor(out=pick[:, t, 0:E], in0=rows_f[:, 0:E], scalar=iota_c[:, t:t + 1],
                                             in1=pick[:, t, E:2 * E].bitcast(F32), op0=ALU.is_equal, op1=ALU.add)
                for t in range(ET):
                    dve.tensor_scalar(onesrc[:, t, :], iota_row, sorted_c[:, t, 0:1], None, ALU.is_equal)
                for h in range(H):
                    rows = slice(h * DH, (h + 1) * DH)
                    ins = dve.tensor_scalar(apad[rows, h::BH + H], ones[rows, 0:CB], a_c[rows, :], None, ALU.mult)
                link(ins)
                dve.sem_inc(tv_free, 1)

            def make_r():
                dve.wait_ge(m_ready, 1)
                for k in range(STEPS):
                    i = STEPS - k - 1
                    ins = dve.tensor_scalar(r_k(k), att[1 - i // 4][:, (i % 4) * D:(i % 4 + 1) * D], float(comb(STEPS, k)), None, ALU.mult)
                link(ins)
                dve.sem_inc(m_copied, 1)
                for i in range(STEPS):
                    for k in range(STEPS - i):
                        coef = DT * comb(i + k, k) + (1.0 if i == 0 and k == 0 else 0.0)
                        ins = dve.scalar_tensor_tensor(out=r_k(k), in0=qp[:, i, :], scalar=coef, in1=r_k(k), op0=ALU.mult, op1=ALU.add)
                    link(ins)
                dve.sem_inc(r_done, 1)

            def stage(col, n, ps):
                hi, lo = slice(col, col + n), slice(col + BABY, col + BABY + n)
                link(dve.tensor_copy(staged[:, :, hi], ps))
                link(dve.tensor_tensor(staged[:, :, lo], ps, staged[:, :, hi].bitcast(F32), ALU.subtract))
                dve.sem_inc(u_staged, 1)

            def u_copy(s):
                dve.wait_ge(u_ready, s + 1)
                rows = slice(ROW(s), ROW(s) + 2 * BABY)
                link(dve.tensor_copy(urows[rows, :], att[1][rows, :]))
                if s == 1:
                    dve.wait_ge(u012_turned, 1)
                    link(dve.tensor_copy(urows[0:2 * BABY, :], att[0][0:2 * BABY, :]))
                dve.sem_inc(u_rows, 1)

            def xt_lo(c, b):
                dve.wait_ge(xt_hi, CB * c + b + 1)
                dve.tensor_tensor(ktl[:, b % 2, 0, :], xt_bank(b)[:, :], kth[:, b % 2, 0, :].bitcast(F32), ALU.subtract).then_inc(xt_free, 1)

            def baby_lo(c, b, j):
                dve.wait_ge(left_hi, 2 * CB * c + 2 * b + j)
                dve.tensor_tensor(ktl[:, b % 2, j, :], left[(j - 1) % 2][:, :], kth[:, b % 2, j, :].bitcast(F32),
                                  ALU.subtract).then_inc(left_free, 1)

            def y_split(c, b, p, with_bias):
                dve.wait_ge(y_copied, R_JOBS * c + PAIRS * b + p + 1)
                ps = yps[:, 2 * p:2 * p + 2, :]
                rows, cols = slice(2 * p, 2 * p + 2), slice(b * D, (b + 1) * D)
                dve.tensor_tensor(y2l[:, rows, cols], ps[:, :, 2 * D:3 * D], y2h[:, rows, cols].bitcast(F32), ALU.subtract)
                if with_bias:
                    dve.tensor_tensor(y0[:, rows, cols], ps[:, :, 0:D], bias[:, rows, :], ALU.add).then_inc(y_free, 1)
                else:
                    dve.tensor_copy(y0[:, rows, cols], ps[:, :, 0:D]).then_inc(y_free, 1)

            def s_add(c, t):
                job = S_JOB + t
                dve.wait_ge(left_ready, LEFT_JOBS * c + job + 1)
                dve.tensor_tensor(y1[:, t, :], left[job % 2][:, :], y1[:, t, :], ALU.add).then_inc(left_free, 1)

            def s_split(c, t):
                dve.wait_ge(s_hi, NT * c + t + 1)
                dve.tensor_tensor(sl[:, t, :], y1[:, t, :], sh[:, t, :].bitcast(F32), ALU.subtract).then_inc(s_lo, 1)

            def gather_lo(cc, b, bank, hi, lo):
                dve.wait_ge(g_hi, CB * cc + b + 1)
                dve.tensor_tensor(lo, bank, hi.bitcast(F32), ALU.subtract).then_inc(g_lo, 1)

            def leaky(cc, p, bank):
                dve.wait_ge(q_scaled, 2 * cc + p + 1)
                dve.tensor_tensor(tt[:, 2 * p:2 * p + 2, :], bank[:, :].rearrange("p (b e) -> p b e", b=2),
                                  tt[:, 2 * p:2 * p + 2, :], ALU.max).then_inc(q_leaky, 1)

            def attend_values(cc, p, bank):
                dve.wait_ge(head_ready, 2 * cc + p + 1)
                v = vv[:, 2 * p:2 * p + 2, :].rearrange("p b e -> p (b e)")
                dve.tensor_tensor(v, bank, v, ALU.mult).then_inc(av_ready, 1)

            def u_lo(cc, t):
                dve.wait_ge(u2_hi, ET * cc + t + 1)
                dve.tensor_tensor(ul[:, t, :], att[t][:, :], uh[:, t, :].bitcast(F32), ALU.subtract).then_inc(u2_lo, 1)

            def out_add(cc, t):
                job = OUT_JOB + t
                dve.wait_ge(left_ready, LEFT_JOBS * cc + job + 1)
                dve.tensor_tensor(x1[:, t, :], left[job % 2][:, :], y0[:, t, :], ALU.add).then_inc(left_free, 1)
                dve.wait_ge(left_free, LEFT_JOBS * cc + job + 1)

            def z_add(cc, t, bank):
                dve.wait_ge(z_ready, NT * cc + t + 1)
                dve.tensor_tensor(r2[:, t, :], bank, x1[:, t, :], ALU.add).then_inc(z_sum, 1)
                dve.wait_ge(z_sum, NT * (cc + 1) + t + 1)

            def stats(k, cc, t, rows):
                for b in range(CB):
                    ins = dve.bn_stats(st[:, k, t, b, :], rows[:, b * D:(b + 1) * D])
                ins.then_inc(ln_stats[k], 1)

            def moments(k, cc, t, n):
                dve.wait_ge(ln_stats[k], NT * cc + t + n)
                dve.sem_inc(ln_turn[k], 1)
                for i in range(t, t + n):
                    for b in range(CB):
                        ins = dve.bn_aggr(moment[:, k, i, b, :], st[:, k, i, b, :])
                ins.then_inc(ln_var[k], n)

            def normalise(k, cc, t, tiles, bank=None):
                dve.wait_ge(ln_rstd[k], NT * cc + t + 1)
                for b in range(CB):
                    cols = slice(b * D, (b + 1) * D)
                    ins = dve.tensor_scalar(tiles[:, t, cols], (tiles[:, t, cols] if bank is None else bank[:, cols]),
                                            moment[:, k, t, b, 0:1], rstd[:, k, t, b:b + 1], ALU.add, ALU.mult)
                ins.then_inc(ln_dve[k], 1)

            def x1_split(cc, t, hi, lo, done):
                dve.wait_ge(x1_hi, NT * cc + t + 1)
                dve.tensor_tensor(lo[:, t, :], x1[:, t, :], hi[:, t, :].bitcast(F32), ALU.subtract).then_inc(done, 1)

            def sm(cc, n, ins):
                ins.then_inc(sm_step, 1)
                dve.wait_ge(sm_step, SM * cc + n)

            def softmax_max(cc, bank):
                dve.wait_ge(score_ready, cc + 1)
                sm(cc, 1, dve.tensor_tensor(sme[:, :], bank, logrow[:, :], ALU.add))
                sm(cc, 2, dve.tensor_tensor_scan(smf[:, :], seg[:, 0:E], sme[:, :], LOWEST, ALU.add, ALU.max))
                sm(cc, 3, dve.tensor_tensor_scan(smg[:, ::-1], seg[:, E:0:-1], smf[:, ::-1], LOWEST, ALU.add, ALU.max))
                dve.tensor_tensor(smg[:, :], sme[:, :], smg[:, :], ALU.subtract).then_inc(sm_step, 1)

            def softmax_sum(cc):
                dve.wait_ge(sm_exp, cc + 1)
                sm(cc, 5, dve.tensor_tensor_scan(smg[:, :], same[:, :], smf[:, :], 0.0, ALU.mult, ALU.add))
                sm(cc, 6, dve.tensor_tensor_scan(sme[:, ::-1], seg[:, E:0:-1], smg[:, ::-1], LOWEST, ALU.add, ALU.max))
                sm(cc, 7, dve.reciprocal(smg[:, :], sme[:, :]))
                dve.tensor_tensor(attn_h[:, :], smf[:, :], smg[:, :], ALU.mult)
                sm(cc, 8, dve.tensor_tensor(sme[:, :], smf[:, :], smg[:, :], ALU.mult))
                dve.tensor_tensor(attn_l[:, :], sme[:, :], attn_h[:, :].bitcast(F32), ALU.subtract).then_inc(attn_ready, 1)

            def body(c, attend):
                head = not attend
                if attend:
                    out_add(c - 1, 0)
                    stats(0, c - 1, 0, x1[:, 0, :])
                    out_add(c - 1, 1)
                    stats(0, c - 1, 1, x1[:, 1, :])
                    moments(0, c - 1, 0, 2)
                    out_add(c - 1, 2)
                    stats(0, c - 1, 2, x1[:, 2, :])
                    out_add(c - 1, 3)
                    stats(0, c - 1, 3, x1[:, 3, :])
                    moments(0, c - 1, 2, 2)
                if head:
                    dve.wait_ge(x_loaded, 16 * NT)
                    dve.tensor_copy(xh[:, 0, :, :], xraw[:, :, 0:D]).then_inc(x_hi, 1)
                    dve.wait_ge(x_hi, 1)
                    dve.tensor_tensor(xl[:, 0, :, :], xraw[:, :, 0:D], xh[:, 0, :, :].bitcast(F32), ALU.subtract).then_inc(x_lo, 1)
                    power_lo(0, p1h, p1l)
                    for t in (0, 2):
                        dve.wait_ge(pn_hi, t + 1)
                        dve.tensor_tensor(pnl[:, t, :], pn[:, t, :], pnh[:, t, :].bitcast(F32), ALU.subtract).then_inc(pn_lo, 1)
                    baby_lo(c, 0, 1)
                    for t in range(NT):
                        ins = dve.tensor_reduce(u012[:, t, 1:2], pn[:, t, :], mybir.AxisListType.X, ALU.add)
                    link(ins)
                    dve.memset(urows, 0.0)
                    rank_edges()
                    stage(ROW(0), 1, u012[:, :, 1:2])
                    power_lo(1, p2h, p2l)
                    baby_lo(c, 0, 2)
                    make_r()
                    power_lo(2, p3h, p3l)
                    dve.wait_ge(r_hi, 1)
                    dve.tensor_tensor(rl[:, :, :].rearrange("p j e -> p (j e)"), rf[:, :, :, :].rearrange("p j i e -> p (j i e)"),
                                      rh[:, :, :].rearrange("p j e -> p (j e)").bitcast(F32), ALU.subtract).then_inc(r_lo, 1)
                    xt_lo(c, 0)
                    xt_lo(c, 1)
                else:
                    xt_lo(c, 0)
                    x1_split(c - 1, 0, x1h, x1l, x1_lo)
                    baby_lo(c, 0, 1)
                    baby_lo(c, 0, 2)
                    normalise(0, c - 1, 3, x1)
                    x1_split(c - 1, 1, x1h, x1l, x1_lo)
                    xt_lo(c, 1)
                    x1_split(c - 1, 2, x1h, x1l, x1_lo)
                    x1_split(c - 1, 3, x1h, x1l, x1_lo)
                baby_lo(c, 1, 1)
                baby_lo(c, 1, 2)
                if head:
                    edge_index()
                if attend:
                    gather_lo(c - 1, 0, att[0][:, :], gh[:, 0, :], gl[:, 0, :])
                    gather_lo(c - 1, 1, att[1][:, :], gh[:, 1, :], gl[:, 1, :])
                y_split(c, 0, 0, attend)
                y_split(c, 0, 1, attend)
                if head:
                    edge_onehots()
                if attend:
                    leaky(c - 1, 0, att[0])
                baby_lo(c, 2, 1)
                xt_lo(c, 2)
                if attend:
                    gather_lo(c - 1, 2, att[0][:, :], gh[:, 0, :], gl[:, 0, :])
                    gather_lo(c - 1, 3, att[1][:, :], gh[:, 1, :], gl[:, 1, :])
                baby_lo(c, 2, 2)
                if head:
                    dve.wait_ge(c_turned, 1)
                    dve.tensor_copy(c_rows, att[0][:, 0:P])
                    u_copy(0)
                else:
                    leaky(c - 1, 1, att[0])
                y_split(c, 1, 0, attend)
                if attend:
                    softmax_max(c - 1, att[0][0:BH, 0:E])
                    softmax_sum(c - 1)
                y_split(c, 1, 1, attend)
                if head:
                    dve.wait_ge(u_turned, 1)
                    link(dve.tensor_copy(u012[:, :, 2:3], att[0][:, 0:NT].rearrange("p (t n) -> p t n", n=1)))
                    stage(ROW(1), BABY, u012[:, :, 0:BABY])
                xt_lo(c, 3)
                baby_lo(c, 3, 1)
                baby_lo(c, 3, 2)
                if head:
                    u_copy(1)
                if attend:
                    for p in range(2):
                        attend_values(c - 1, p, att[p][:, :])
                y_split(c, 2, 0, attend)
                y_split(c, 2, 1, attend)
                if head:
                    dve.wait_ge(u_turned, 2)
                    stage(ROW(2), BABY, att[0][:, 0:BABY * NT].rearrange("p (t n) -> p t n", n=BABY))
                    dve.wait_ge(logs, 1)
                    for t in range(ET):
                        ins = dve.tensor_scalar(log_rep[:, t, :], ones[:, 0:BH], log_c[:, t:t + 1], None, ALU.mult)
                    ins.then_inc(log_rep_ready, 1)
                if attend:
                    for t in range(ET):
                        u_lo(c - 1, t)
                y_split(c, 3, 0, attend)
                y_split(c, 3, 1, attend)
                if head:
                    u_copy(2)
                if attend:
                    z_add(c - 1, 0, att[0][:, :])
                    z_add(c - 1, 1, att[1][:, :])
                    stats(1, c - 1, 0, r2[:, 0, :])
                s_add(c, 0)
                if attend:
                    stats(1, c - 1, 1, r2[:, 1, :])
                s_split(c, 0)
                s_add(c, 1)
                if attend:
                    moments(1, c - 1, 0, 2)
                s_split(c, 1)
                if head:
                    dve.wait_ge(log_row_ready, 1)
                    dve.tensor_copy(logrow[:, :], att[0][0:BH, 0:E])
                s_add(c, 2)
                if attend:
                    z_add(c - 1, 2, att[0][:, :])
                s_split(c, 2)
                if attend:
                    stats(1, c - 1, 2, r2[:, 2, :])
                s_add(c, 3)
                s_split(c, 3)
                if attend:
                    z_add(c - 1, 3, att[1][:, :])
                    stats(1, c - 1, 3, r2[:, 3, :])
                    moments(1, c - 1, 2, 2)
                if head:
                    dve.wait_ge(bias_ready, 1)
                    link(dve.tensor_copy(bias[:, :, :].rearrange("p t e -> p (t e)"), att[1][:, :]))
                    dve.sem_inc(z_sum, NT)
                    for t in range(NT):
                        row = y0[:, t, :].rearrange("p (b e) -> p b e", b=CB)
                        ins = dve.tensor_tensor(row, row, bias[:, t:t + 1, :].broadcast_to([P, CB, D]), ALU.add)
                    link(ins)

            def tail(cc):
                for t in range(NT):
                    out_add(cc, t)
                    stats(0, cc, t, x1[:, t, :])
                    moments(0, cc, t, 1)
                    if t == 1:
                        normalise(0, cc, 0, x1)
                x1_split(cc, 1, y2h, y2l, x1_last)
                normalise(0, cc, 3, x1)
                x1_split(cc, 2, y2h, y2l, x1_last)
                x1_split(cc, 3, y2h, y2l, x1_last)
                for b in range(CB):
                    gather_lo(cc, b, yps[:, b, :], *((gh[:, b, :], gl[:, b, :]) if b < 2 else (kth[:, 0, b - 2, :], ktl[:, 0, b - 2, :])))
                leaky(cc, 0, att[0])
                leaky(cc, 1, left[0])
                softmax_max(cc, yps[0:BH, 0, 0:E])
                softmax_sum(cc)
                for p in range(2):
                    attend_values(cc, p, yps[:, 1 + p, :])
                for p in range(2):
                    dve.wait_ge(av_hi, 2 * cc + p + 1)
                    dve.tensor_tensor(avl[:, 2 * p:2 * p + 2, :], vv[:, 2 * p:2 * p + 2, :],
                                      avh[:, 2 * p:2 * p + 2, :].bitcast(F32), ALU.subtract).then_inc(av_lo, 1)
                for t in range(ET):
                    u_lo(cc, t)
                for t in range(NT):
                    dve.wait_ge(z_ready, NT * cc + t + 1)
                    stats(1, cc, t, last_bank(t))
                    moments(1, cc, t, 1)
                for t in range(PAIRS, NT):
                    normalise(1, cc, t, r2, last_bank(t))

            chunks(dve, body, tail)


_INS = ['x', 'adj', 'L0_gnn_alpha_train', 'L0_gnn_w', 'L0_gnn_d', 'L0_gnn_fc_in_w', 'L0_gnn_fc_in_b', 'L1_gnn_W_lin',
        'L1_gnn_W_val', 'L1_gnn_a', 'L1_gnn_W_out', 'L1_gnn_src', 'L1_gnn_dst']
_OUTS = [((16, 512, 128), 'float32')]


def kernel(**inputs):
    import numpy as _np
    import concourse.bacc as _bacc
    from concourse import mybir as _mybir
    from concourse.bass_utils import run_bass_kernel_spmd as _run

    nc = _bacc.Bacc("TRN2", target_bir_lowering=False, num_devices=1)
    arrays, args = {}, []
    for name in _INS:
        a = _np.ascontiguousarray(inputs[name])
        arrays[f"in_{name}_dram"] = a
        args.append(nc.dram_tensor(f"in_{name}_dram", a.shape, _mybir.dt.from_np(a.dtype), kind="ExternalInput").ap())
    for i, (shape, dtype) in enumerate(_OUTS):
        dt = _mybir.dt.from_np(_np.dtype(dtype))
        args.append(nc.dram_tensor(f"out_{i}_dram", shape, dt, kind="ExternalOutput").ap())
    graph_kernel(nc, *args)
    r = _run(nc, [arrays], core_ids=[0])
    got = tuple(r.results[0][f"out_{i}_dram"] for i in range(len(_OUTS)))
    return got[0]
```
